# Optimizing a Trainium2 kernel written in Bass

```python
import numpy as np
import jax
import jax.numpy as jnp

def _softmax(x, axis=-1):
    return jax.nn.softmax(x, axis=axis)

def _gelu(x):
    return jax.nn.gelu(x, approximate=True)

def _silu(x):
    return jax.nn.silu(x)

def _sigmoid(x):
    return jax.nn.sigmoid(x)

def _layernorm(x, axis=-1, eps=1e-05):
    m = jnp.mean(x, axis=axis, keepdims=True)
    v = jnp.var(x, axis=axis, keepdims=True)
    return (x - m) / jnp.sqrt(v + eps)

def _scatter_add(tgt, idx, src, axis=0):
    return tgt.at[idx].add(src)

def _segment_sum(src, seg, n):
    return jax.ops.segment_sum(src, seg, n)
kernel_name = 'mk_vit_tower_d1_tok_img768_r4_dad0ba'

def setup_inputs(seed: int=0):
    np.random.seed(seed)
    _w = jnp.asarray

    def _rec_inputs():
        import jax
        import jax.numpy as jnp
        _rk = jax.random.key(seed)
        x = -0.000222058 + 0.999998 * jax.random.normal(jax.random.fold_in(_rk, 1), (16, 128, 192, 1), jnp.float32)
        return x
    x = _rec_inputs()

    def _L0_tok_setup():
        import jax, jax.numpy as jnp
        from jax import lax
        import numpy as np
        DIM = 192
        K = 7
        PAD = K // 2
        EPS = 1e-06
        key = jax.random.key(seed)
        ks = jax.random.split(key, 6)
        B, L = (64, 128)
        x = jax.random.normal(ks[0], (B, L, DIM, 1), dtype=jnp.float32)
        fan_dw = 1 * K * 1
        dw_w = jax.random.uniform(ks[1], (DIM, 1, K, 1), jnp.float32, -1.0 / np.sqrt(fan_dw), 1.0 / np.sqrt(fan_dw))
        fan_pw = DIM
        pw_w = jax.random.uniform(ks[2], (DIM, DIM), jnp.float32, -1.0 / np.sqrt(fan_pw), 1.0 / np.sqrt(fan_pw))
        pw_b = jax.random.uniform(ks[3], (DIM,), jnp.float32, -1.0 / np.sqrt(fan_pw), 1.0 / np.sqrt(fan_pw))
        ln_g = jnp.ones((DIM,), jnp.float32)
        ln_b = jnp.zeros((DIM,), jnp.float32)
        return {'x': x, 'dw_w': dw_w, 'pw_w': pw_w, 'pw_b': pw_b, 'ln_g': ln_g, 'ln_b': ln_b}
    _L0_tok_all = _L0_tok_setup()
    _L0_tok_in = {k: v for k, v in _L0_tok_all.items() if k in ('dw_w', 'pw_w', 'pw_b', 'ln_g', 'ln_b')}
    del _L0_tok_all

    def _L0_attn_setup():
        import jax, jax.numpy as jnp
        import numpy as np
        B, S, D, H = (8, 256, 192, 12)
        HS = D // H
        key = jax.random.key(seed)
        k1, k2, k3 = jax.random.split(key, 3)
        x = jax.random.normal(k1, (B, S, D), dtype=jnp.float32)
        W_attn = jax.random.normal(k2, (D, 3 * H * HS), dtype=jnp.float32) * 0.02
        b_attn = jnp.zeros((3 * H * HS,), dtype=jnp.float32)
        W_proj = jax.random.normal(k3, (H * HS, D), dtype=jnp.float32) * 0.02
        b_proj = jnp.zeros((D,), dtype=jnp.float32)
        return {'x': x, 'W_attn': W_attn, 'b_attn': b_attn, 'W_proj': W_proj, 'b_proj': b_proj}
    _L0_attn_all = _L0_attn_setup()
    _L0_attn_in = {k: v for k, v in _L0_attn_all.items() if k in ('W_attn', 'b_attn', 'W_proj', 'b_proj')}
    del _L0_attn_all

    def _L0_ffn_setup():
        import math
        import jax, jax.numpy as jnp
        import numpy as np
        NUM_EXPERTS = 8
        TOP_K = 2
        CAPACITY_FACTOR = 1.25
        H = 192
        INNER = 768
        B, S = (2, 512)
        key = jax.random.key(seed)
        ks = jax.random.split(key, 9)
        scale = 0.02
        x = jax.random.normal(ks[0], (B, S, H), dtype=jnp.float32)
        Wr = jax.random.normal(ks[1], (H, NUM_EXPERTS), dtype=jnp.float32) * scale
        w1 = jax.random.normal(ks[2], (NUM_EXPERTS, H, INNER), dtype=jnp.float32) * scale
        w3 = jax.random.normal(ks[3], (NUM_EXPERTS, H, INNER), dtype=jnp.float32) * scale
        w2 = jax.random.normal(ks[4], (NUM_EXPERTS, INNER, H), dtype=jnp.float32) * scale
        s1 = jax.random.normal(ks[5], (H, INNER), dtype=jnp.float32) * scale
        s3 = jax.random.normal(ks[6], (H, INNER), dtype=jnp.float32) * scale
        s2 = jax.random.normal(ks[7], (INNER, H), dtype=jnp.float32) * scale
        return {'x': x, 'Wr': Wr, 'w1': w1, 'w3': w3, 'w2': w2, 's1': s1, 's3': s3, 's2': s2}
    _L0_ffn_all = _L0_ffn_setup()
    _L0_ffn_in = {k: v for k, v in _L0_ffn_all.items() if k in ('Wr', 'w1', 'w3', 'w2', 's1', 's3', 's2')}
    del _L0_ffn_all
    return {'x': x, 'L0_tok_dw_w': _L0_tok_in['dw_w'], 'L0_tok_pw_w': _L0_tok_in['pw_w'], 'L0_tok_pw_b': _L0_tok_in['pw_b'], 'L0_tok_ln_g': _L0_tok_in['ln_g'], 'L0_tok_ln_b': _L0_tok_in['ln_b'], 'L0_attn_W_attn': _L0_attn_in['W_attn'], 'L0_attn_b_attn': _L0_attn_in['b_attn'], 'L0_attn_W_proj': _L0_attn_in['W_proj'], 'L0_attn_b_proj': _L0_attn_in['b_proj'], 'L0_ffn_Wr': _L0_ffn_in['Wr'], 'L0_ffn_w1': _L0_ffn_in['w1'], 'L0_ffn_w3': _L0_ffn_in['w3'], 'L0_ffn_w2': _L0_ffn_in['w2'], 'L0_ffn_s1': _L0_ffn_in['s1'], 'L0_ffn_s3': _L0_ffn_in['s3'], 'L0_ffn_s2': _L0_ffn_in['s2']}

def reference(x, L0_tok_dw_w, L0_tok_pw_w, L0_tok_pw_b, L0_tok_ln_g, L0_tok_ln_b, L0_attn_W_attn, L0_attn_b_attn, L0_attn_W_proj, L0_attn_b_proj, L0_ffn_Wr, L0_ffn_w1, L0_ffn_w3, L0_ffn_w2, L0_ffn_s1, L0_ffn_s3, L0_ffn_s2):
    import jax
    import jax.numpy as jnp

    def _L0_tok_ref(x, dw_w, pw_w, pw_b, ln_g, ln_b):
        import jax, jax.numpy as jnp
        from jax import lax
        import numpy as np
        DIM = 192
        K = 7
        PAD = K // 2
        EPS = 1e-06
        h = jnp.transpose(x, (0, 2, 1, 3))
        h = lax.conv_general_dilated(h, dw_w, window_strides=(1, 1), padding=((PAD, PAD), (0, 0)), dimension_numbers=('NCHW', 'OIHW', 'NCHW'), feature_group_count=DIM)
        h = h[..., 0]
        y = jnp.einsum('bdl,ed->ble', h, pw_w) + pw_b
        mu = jnp.mean(y, axis=-1, keepdims=True)
        var = jnp.mean(jnp.square(y - mu), axis=-1, keepdims=True)
        y = (y - mu) * lax.rsqrt(var + EPS) * ln_g + ln_b
        return jax.nn.relu(y)

    def _L0_attn_ref(x, W_attn, b_attn, W_proj, b_proj):
        import jax, jax.numpy as jnp
        import numpy as np
        B, S, D, H = (8, 256, 192, 12)
        HS = D // H
        b, s, d = x.shape
        qkv = (x @ W_attn + b_attn).reshape(b, s, 3, H, HS)
        q, k, v = (qkv[:, :, 0], qkv[:, :, 1], qkv[:, :, 2])
        scale = jnp.sqrt(jnp.asarray(HS, dtype=x.dtype))
        scores = jnp.einsum('bqhd,bkhd->bhqk', q, k) / scale
        causal = jnp.tril(jnp.ones((s, s), dtype=bool))
        scores = jnp.where(causal, scores, -jnp.inf)
        attn = jax.nn.softmax(scores, axis=-1)
        out = jnp.einsum('bhqk,bkhd->bqhd', attn, v).reshape(b, s, H * HS)
        return out @ W_proj + b_proj

    def _L0_ffn_ref(x, Wr, w1, w3, w2, s1, s3, s2):
        import math
        import jax, jax.numpy as jnp
        import numpy as np
        NUM_EXPERTS = 8
        TOP_K = 2
        CAPACITY_FACTOR = 1.25
        H = 192
        INNER = 768
        B, S = (2, 512)
        b, s, h = x.shape
        n = b * s
        flat = x.reshape(n, h)
        logits = flat @ Wr
        probs = jax.nn.softmax(logits, axis=-1)
        topk_p, topk_i = jax.lax.top_k(probs, TOP_K)
        topk_p = topk_p / jnp.clip(topk_p.sum(-1, keepdims=True), 1e-09)
        capacity = max(1, math.ceil(n * TOP_K / NUM_EXPERTS * CAPACITY_FACTOR))
        onehot = topk_i[None, :, :] == jnp.arange(NUM_EXPERTS)[:, None, None]
        w_tok = jnp.sum(topk_p[None] * onehot, axis=-1)
        assigned = jnp.any(onehot, axis=-1)
        score = jnp.where(assigned, w_tok, -jnp.inf)
        order = jnp.argsort(-score, axis=1)[:, :capacity]
        score_sel = jnp.take_along_axis(score, order, axis=1)
        valid = jnp.isfinite(score_sel)
        weight_sel = jnp.where(valid, score_sel, 0.0)
        dispatch = flat[order]
        gate = jax.nn.silu(jnp.einsum('ech,ehi->eci', dispatch, w1))
        up = jnp.einsum('ech,ehi->eci', dispatch, w3)
        expert_out = jnp.einsum('eci,eih->ech', gate * up, w2)
        expert_out = expert_out * weight_sel[..., None]
        routed = jnp.zeros((n, h), dtype=flat.dtype)
        routed = routed.at[order.reshape(-1)].add(expert_out.reshape(-1, h))
        shared = jax.nn.silu(flat @ s1) * (flat @ s3) @ s2
        out = routed + shared
        return out.reshape(b, s, h)
    h = _L0_tok_ref(x, L0_tok_dw_w, L0_tok_pw_w, L0_tok_pw_b, L0_tok_ln_g, L0_tok_ln_b)
    h = h + _L0_attn_ref(_layernorm(h, axis=-1), L0_attn_W_attn, L0_attn_b_attn, L0_attn_W_proj, L0_attn_b_proj)
    h = h + _L0_ffn_ref(_layernorm(h, axis=-1), L0_ffn_Wr, L0_ffn_w1, L0_ffn_w3, L0_ffn_w2, L0_ffn_s1, L0_ffn_s3, L0_ffn_s2)
    return h

_drawn_inputs = setup_inputs


def setup_inputs(seed=0):
    import zlib

    import numpy as np

    out = dict(_drawn_inputs(seed))
    spreads = {'L0_tok_ln_g': (1.0, 0.2),
     'L0_tok_ln_b': (0.0, 0.1),
     'L0_attn_b_attn': (0.0, 0.1),
     'L0_attn_b_proj': (0.0, 0.1)}
    factors = {'L0_ffn_Wr': 3.151, 'L0_ffn_w1': 2.827, 'L0_ffn_w3': 2.801, 'L0_ffn_w2': 2.812}
    for name, (base, spread) in spreads.items():
        noise = np.random.default_rng([zlib.crc32(name.encode()), seed]).standard_normal(out[name].shape)
        drawn = base * np.exp(spread * noise) if base else spread * noise
        out[name] = jnp.asarray(drawn.astype(out[name].dtype))
    for name, factor in factors.items():
        out[name] = (out[name] * factor).astype(out[name].dtype)
    return out
```

```python
from contextlib import ExitStack

import concourse.bass as bass
from concourse import mybir

ALU = mybir.AluOpType
ACT = mybir.ActivationFunctionType
AX = mybir.AxisListType
F32 = mybir.dt.float32
BF16 = mybir.dt.bfloat16
I32 = mybir.dt.int32
RADD = bass.bass_isa.ReduceOp.add

NB, L, D = 16, 128, 192
N = NB * L
DC = 96
TAPS = 7
NH, HS = 12, 16
HG = 3
NG = NH // HG
NE, INNER = 8, 768
IC = INNER // 128
CAP = (N * 2 * 5 // 4) // NE
CT = CAP // 128
HALF = CAP // 2
GT = 4
GN = GT * L
NEG = -1.0e30
ACTIVE = range(-4, NB + 1)
FIRST, LAST = 2, 11
BITS = 30


class Tile:

    def __init__(self, const, reg=None):
        self.const, self.reg = const, reg

    def __add__(self, k):
        return Tile(self.const + k, self.reg)

    @property
    def v(self):
        return self.const if self.reg is None else self.reg * 2 + self.const

    @property
    def pair(self):
        return self.const // 2 if self.reg is None else self.reg + self.const // 2

    @property
    def parity(self):
        return self.const % 2

    def inside(self):
        return self.reg is not None or 0 <= self.const < NB

    def after(self, k):
        return self.reg is not None or self.const >= k


def vit_tower(nc, xT, dw, pwT, pw_b, ln_g, ln_b, wqkv, b_attn, wproj, b_proj, wr, w1, w3, w2,
              s1, s3, s2, out):
    with ExitStack() as ctx:
        def sb(name, shape, dt=F32):
            return ctx.enter_context(nc.sbuf_tensor(name, shape, dt))

        def ps(name, shape, dt=F32):
            return ctx.enter_context(nc.psum_tensor(name, shape, dt))

        def sem(name):
            return ctx.enter_context(nc.semaphore(name))

        slots_in = nc.dram_tensor("slots_in", [NE * CAP + 2 * N, D], F32).ap()
        slots_out = nc.dram_tensor("slots_out", [NE * CAP, D], F32).ap()

        xb = sb("xb", [DC, 2, 2, L + TAPS - 1])
        dw_sb = sb("dw_sb", [DC, 2, TAPS])
        cv = sb("cv", [DC + 1, 2, 2, L])
        pw_sb = sb("pw_sb", [DC + 1, 2, D])
        g_bc = sb("g_bc", [128, D])
        b_bc = sb("b_bc", [128, D])
        bproj_bc = sb("bproj_bc", [128, D])
        wqkv_sb = sb("wqkv_sb", [DC + 1, 2, 3 * D])
        wproj_sb = sb("wproj_sb", [128, HG, D])
        wr_sb = sb("wr_sb", [DC, 2, NE])
        ident = sb("ident", [128, 128])
        identb = sb("identb", [128, 128], BF16)
        causal = sb("causal", [128, HG, L], BF16)
        headmask = sb("headmask", [DC, 6])
        tri = sb("tri", [128, 128])
        ones = sb("ones", [128, 128])
        eps1 = sb("eps1", [128, 1])
        eps2 = sb("eps2", [128, 1])
        mhalf = sb("mhalf", [128, 1])
        st = sb("st", [128, 3, 6])
        mv = sb("mv", [128, 3, 2])
        ve = sb("ve", [128, 3, 1])
        rstd = sb("rstd", [128, 3, 1])
        carry = sb("carry", [128, 3])
        tn = sb("tn", [128, D])
        un = sb("un", [128, D])
        h1 = sb("h1", [128, D])
        xn = sb("xn", [128, D])
        xnT = sb("xnT", [DC + 1, 2, L])
        qT = sb("qT", [DC, 2, L])
        kbd = sb("kbd", [DC, 2, 6, L])
        vs = sb("vs", [128, 2, NH, 32])
        probs = sb("probs", [128, NG, HG, L])
        nmax = sb("nmax", [128, NH])
        rsum = sb("rsum", [128, NH])
        rinv = sb("rinv", [128, NH])
        pT = sb("pT", [128, NH, L])
        oT = sb("oT", [128, HG, L])
        H = sb("H", [128, NB, D])
        hrow = sb("hrow", [128, D])
        xn2s = sb("xn2s", [128, D])
        xn2 = sb("xn2", [128, NB, D])
        xn2T = sb("xn2T", [DC, 2, N])
        edesc = sb("edesc", [128, NB, NE])
        ebase = sb("ebase", [128, NB, NE])
        dump = sb("dump", [128, 2, NB])
        RT = [sb(f"rt{i}", [128, NB, NE]) for i in range(8)]
        RS = [sb(f"rs{i}", [128, NB]) for i in range(4)]
        score = sb("score", [128, NB, NE])
        oh = sb("oh", [128, 2, NB, NE])
        wgt = sb("wgt", [128, 2, NB])
        thr = sb("thr", [128, NE], I32)
        cand = sb("cand", [128, NE], I32)
        bit = sb("bit", [128, NE], I32)
        cnt = sb("cnt", [128, NE])
        tot = sb("tot", [128, NE])
        ge = sb("ge", [128, NE], I32)
        dst_i = sb("dst_i", [128, 2, NB], I32)
        src_i = sb("src_i", [128, 2, NB], I32)
        segm = sb("segm", [128, NE, NB])
        W1 = sb("W1", [DC, 2, 2, INNER])
        W3 = sb("W3", [DC, 2, 2, INNER])
        W2 = sb("W2", [128, 2, IC, D])
        S1 = sb("S1", [DC, 2, INNER])
        S3 = sb("S3", [DC, 2, INNER])
        S2 = sb("S2", [128, IC, D])
        sg = pT[:, 0:8].rearrange("p (s h) n -> p s (h n)", s=2)
        G = sb("G", [128, IC, CAP])
        xg = sb("xg", [128, 2, CT, D])
        xgT = sb("xgT", [DC, 2, 2, CAP])
        ys = sb("ys", [128, NE, CT, D])
        lgT = G[0:NE].rearrange("p c n -> p (c n)")[:, 0:N]
        gath = probs[:].rearrange("p g h n -> p (g h n)").rearrange("p (s j d) -> p s j d", s=4, j=2)

        bank_qv = ps("bank_qv", [128, 512])
        bank_k = ps("bank_k", [128, 512])
        bank_s = [ps(f"bank_s{g}", [128, 512]) for g in range(NG)]
        bank_o = ps("bank_o", [128, 512])
        bank_y = ps("bank_y", [128, 512])
        up_a, up_b = bank_s[0:2], bank_s[2:4]
        down = [bank_o, bank_y]
        turn = [bank_qv, bank_k]

        s_x = [sem("s_x0"), sem("s_x1")]
        s_wa = sem("s_wa")
        s_bc = sem("s_bc")
        s_cst = sem("s_cst")
        s_cd = sem("s_cd")
        s_pc = sem("s_pc")
        s_conv = sem("s_conv")
        s_y = sem("s_y")
        s_ln = sem("s_ln")
        s_r1 = sem("s_r1")
        s_r2 = sem("s_r2")
        s_r3 = sem("s_r3")
        s_relu = sem("s_relu")
        s_h1b = sem("s_h1b")
        s_t1 = sem("s_t1")
        s_xnt = sem("s_xnt")
        s_k = sem("s_k")
        s_qvm = sem("s_qvm")
        s_qv = sem("s_qv")
        s_kbd = sem("s_kbd")
        s_s = sem("s_s")
        s_max = sem("s_max")
        s_exp = sem("s_exp")
        s_rinv = sem("s_rinv")
        s_norm = sem("s_norm")
        s_ptm = sem("s_ptm")
        s_pt = sem("s_pt")
        s_pv = sem("s_pv")
        s_o = sem("s_o")
        s_proj = sem("s_proj")
        s_l3 = sem("s_l3")
        s_t2 = sem("s_t2")
        s_xn2t = sem("s_xn2t")
        s_xc = sem("s_xc")
        s_zero = sem("s_zero")
        s_zf = sem("s_zf")
        s_lg = sem("s_lg")
        s_lgc = sem("s_lgc")
        s_lgt = sem("s_lgt")
        s_rt = sem("s_rt")
        s_rex = sem("s_rex")
        s_thr = sem("s_thr")
        s_cnt = sem("s_cnt")
        s_tot = sem("s_tot")
        s_pre = sem("s_pre")
        s_ix = sem("s_ix")
        s_scat = sem("s_scat")
        s_sw = sem("s_sw")
        s_w = [sem("s_w0"), sem("s_w1")]
        s_xg = [sem("s_xg0"), sem("s_xg1")]
        s_u = sem("s_u")
        s_silu = sem("s_silu")
        s_mul = sem("s_mul")
        s_d = sem("s_d")
        s_ye = sem("s_ye")
        s_xt = sem("s_xt")
        s_xte = sem("s_xte")
        s_yst = sem("s_yst")
        s_g = [sem(f"s_g{i}") for i in range(4)]
        s_cmb = sem("s_cmb")
        s_out = sem("s_out")

        N_WA = 6
        FREE = 2
        SH = 3
        U_E0, D_E0 = SH * IC, SH * GT
        U_S3, D_S3 = U_E0 + NE * 2 * IC, D_E0 + NE * CT

        def steps(eng, body):
            for i in ACTIVE:
                if i < FIRST or i > LAST:
                    body(Tile(i))
                elif i == FIRST:
                    with eng.Fori(0, (LAST - FIRST + 1) // 2) as r:
                        body(Tile(FIRST, r))
                        body(Tile(FIRST + 1, r))

        block = ctx.enter_context(nc.Block())

        @block.sync
        def _(sp):
            def load_x(b):
                if b.after(2):
                    sp.wait_ge(s_conv, b.v * 14 - 14)
                sp.dma_start(xb[:, b.parity, :, :], xT[:, :, bass.ds(b.v, 1), :].rearrange(
                    "p c o n -> p c (o n)")).then_inc(s_x[b.parity], 16)

            load_x(Tile(0))
            sp.dma_start(dw_sb[:], dw).then_inc(s_wa, 16)
            load_x(Tile(1))
            sp.dma_start(pw_sb[0:DC], pwT).then_inc(s_wa, 16)
            sp.dma_start(pw_sb[DC:DC + 1, 1, :], pw_b).then_inc(s_wa, 16)
            sp.dma_start(g_bc[:], ln_g.partition_broadcast(128)).then_inc(s_bc, 16)
            sp.dma_start(b_bc[:], ln_b.partition_broadcast(128)).then_inc(s_bc, 16)
            sp.dma_start(wqkv_sb[0:DC], wqkv).then_inc(s_wa, 16)
            sp.dma_start(wqkv_sb[DC:DC + 1, 1, :], b_attn).then_inc(s_wa, 16)
            sp.dma_start(bproj_bc[:], b_proj.partition_broadcast(128)).then_inc(s_bc, 16)
            sp.dma_start(wproj_sb[:], wproj).then_inc(s_wa, 16)
            sp.dma_start(wr_sb[:], wr).then_inc(s_sw, 16)
            for b in range(2, NB):
                load_x(Tile(b))
            sp.wait_ge(s_zf, 1)
            sp.dma_start(slots_in[0:NE * CAP, :].rearrange("(p n) d -> p (n d)", p=128),
                         ys[:].rearrange("p e c d -> p (e c d)")).then_inc(s_zero, 16)
            sp.dma_start(S1[:], s1).then_inc(s_sw, 16)
            sp.dma_start(S3[:], s3).then_inc(s_sw, 16)
            sp.dma_start(S2[:], s2).then_inc(s_sw, 16)

            def load_w(e):
                p = e.parity
                sp.dma_start(W1[:, p], w1[bass.ds(e.v, 1)].rearrange("o p c n -> p (o c) n")).then_inc(s_w[p], 16)
                sp.dma_start(W3[:, p], w3[bass.ds(e.v, 1)].rearrange("o p c n -> p (o c) n")).then_inc(s_w[p], 16)
                sp.dma_start(W2[:, p], w2[bass.ds(e.v, 1)].rearrange("o p c n -> p (o c) n")).then_inc(s_w[p], 16)

            def load_xg(e):
                sp.dma_start(xg[:, e.parity], slots_in[bass.ds(e.v * CAP, CAP), :].rearrange(
                    "(t p) d -> p t d", p=128)).then_inc(s_xg[e.parity], 16)

            load_w(Tile(0))
            load_w(Tile(1))
            sp.wait_ge(s_scat, 16 * 2 * NB)
            load_xg(Tile(0))
            load_xg(Tile(1))

            def expert(e, more):
                if more:
                    sp.wait_ge(s_xt, e.v * CT + CT)
                    load_xg(e + 2)
                sp.wait_ge(s_ye, e.v * CT + (D_E0 + CT + FREE))
                if more:
                    load_w(e + 2)
                sp.dma_start(slots_out[bass.ds(e.v * CAP, CAP), :].rearrange("(t p) d -> p t d", p=128),
                             ys[:, bass.ds(e.v, 1)].rearrange("p o t d -> p (o t) d")).then_inc(s_yst, 16)

            with sp.Fori(0, NE // 2 - 1) as r:
                expert(Tile(0, r), True)
                expert(Tile(1, r), True)
            expert(Tile(NE - 2), False)
            expert(Tile(NE - 1), False)
            for t in range(0, NB, 4):
                sp.wait_ge(s_cmb, 2 * (t + 4))
                sp.dma_start(out[t:t + 4].rearrange("t p d -> p t d"), H[:, t:t + 4, :]).then_inc(s_out, 16)
            sp.wait_ge(s_out, 16 * (NB // 4))

        @block.gpsimd
        def _(pool):
            g = nc.gpsimd
            g.memset(ident[:], 0.0).then_inc(s_pc, 1)
            g.memset(causal[:], 0.0).then_inc(s_pc, 1)
            g.memset(headmask[:], 1.0).then_inc(s_pc, 1)
            g.memset(tri[:], 1.0).then_inc(s_pc, 1)
            g.memset(ones[:], 1.0)
            g.memset(eps1[:], 1e-6)
            g.memset(eps2[:], 1e-5)
            g.memset(mhalf[:], -0.5)
            g.memset(segm[:], 1.0).then_inc(s_pc, 1)
            pool.wait_ge(s_pc, 5)
            g.affine_select(out=ident[:], in_=ident[:], compare_op=ALU.not_equal, fill=1.0, base=0,
                            pattern=[[-1, 128]], channel_multiplier=1).then_inc(s_pc, 1)
            g.affine_select(out=causal[:], in_=causal[:], compare_op=ALU.is_ge, fill=NEG, base=0,
                            pattern=[[0, HG], [-1, L]], channel_multiplier=1)
            g.affine_select(out=headmask[:], in_=headmask[:], compare_op=ALU.is_ge, fill=0.0, base=0,
                            pattern=[[-HS, 6]], channel_multiplier=1).then_inc(s_pc, 1)
            g.affine_select(out=tri[:], in_=tri[:], compare_op=ALU.is_gt, fill=0.0, base=0,
                            pattern=[[1, 128]], channel_multiplier=-1)
            g.affine_select(out=segm[:], in_=segm[:], compare_op=ALU.is_gt, fill=0.0, base=0,
                            pattern=[[0, NE], [1, NB]], channel_multiplier=0)
            pool.wait_ge(s_pc, 7)
            g.affine_select(out=headmask[:], in_=headmask[:], compare_op=ALU.is_ge, fill=0.0, base=HS - 1,
                            pattern=[[HS, 6]], channel_multiplier=-1)
            g.tensor_copy(identb[:], ident[:])
            g.iota(edesc[:], pattern=[[0, NB], [-1, NE]], base=NE, channel_multiplier=0,
                   allow_small_or_imprecise_dtypes=True)
            g.iota(ebase[:], pattern=[[0, NB], [CAP, NE]], base=0, channel_multiplier=0,
                   allow_small_or_imprecise_dtypes=True)
            g.iota(dump[:], pattern=[[N, 2], [L, NB]], base=NE * CAP, channel_multiplier=1,
                   allow_small_or_imprecise_dtypes=True).then_inc(s_cst, 1)
            pool.wait_ge(s_bc, 16 * 3)

            def rsqrt(n, eps, done, b, stats):
                pool.wait_ge(s_l3 if n == 2 else s_ln, stats)
                g.tensor_tensor(ve[:, n], mv[:, n, 1:2], eps[:], ALU.add).then_inc(done, 1)
                pool.wait_ge(done, b.v * 2 + 1)
                g.tensor_tensor(rstd[:, n], ve[:, n], mhalf[:], ALU.pow).then_inc(done, 1)

            def norm(b, k):
                pool.wait_ge(s_rinv, b.v * NG + (k + 1))
                g.tensor_tensor(probs[:, k], probs[:, k],
                                rinv[:, HG * k:HG * (k + 1)].unsqueeze(2).to_broadcast([128, HG, L]),
                                ALU.mult).then_inc(s_norm, 1)

            def step(i):
                b = i
                if b.inside():
                    norm(b, 0)
                n = i + 2
                if n.inside():
                    rsqrt(0, eps1, s_r1, n, n.v * 7 + 2)
                if b.inside():
                    norm(b, 1)
                    norm(b, 2)
                    norm(b, 3)
                if n.inside():
                    rsqrt(1, eps2, s_r2, n, n.v * 7 + 6)
                    pool.wait_ge(s_relu, n.v + 1)
                    g.tensor_tensor(H[:, bass.ds(n.v, 1)].rearrange("p o d -> p (o d)"), h1[:], bproj_bc[:],
                                    ALU.add).then_inc(s_h1b, 1)
                m = i + -1
                if m.inside():
                    rsqrt(2, eps2, s_r3, m, m.v * 4 + 3)
                    g.tensor_copy(H[:, bass.ds(m.v, 1)].rearrange("p o d -> p (o d)"), hrow[:]).then_inc(s_xc, 1)
                    pool.wait_ge(s_l3, m.v * 4 + 4)
                    g.tensor_copy(xn2[:, bass.ds(m.v, 1)].rearrange("p o d -> p (o d)"), xn2s[:]).then_inc(s_xc, 1)

            steps(pool, step)

            for n in range(BITS + 1):
                pool.wait_ge(s_cnt, n + 1)
                g.partition_all_reduce(tot[:], cnt[:], 128, RADD).then_inc(s_tot, 1)

            pool.wait_ge(s_zero, 16)
            pool.wait_ge(s_ix, 1)
            for t in range(NB):
                for j in range(2):
                    pool.indirect_dma_start(slots_in, bass.IndirectOffsetOnAxis(ap=dst_i[:, j, t:t + 1], axis=0),
                                            xn2[:, t, :], None).then_inc(s_scat, 16)
            pool.wait_ge(s_yst, 16 * NE)
            for t in range(NB):
                if t >= 4:
                    pool.wait_ge(s_cmb, 2 * (t - 3))
                for j in range(2):
                    pool.indirect_dma_start(gath[:, t % 4, j], None, slots_out,
                                            bass.IndirectOffsetOnAxis(ap=src_i[:, j, t:t + 1], axis=0),
                                            ).then_inc(s_g[t % 4], 16)

        @block.scalar
        def _(act):
            s = nc.scalar

            def exp(b, k):
                act.wait_ge(s_max, b.v * NG + (k + 1))
                if b.after(1):
                    act.wait_ge(s_ptm, b.v * NG + (k + 1 - NG))
                for h in range(HG):
                    c = HG * k + h
                    last = s.activation(probs[:, k, h], bank_s[k][:, h * L:(h + 1) * L], ACT.Exp,
                                        bias=nmax[:, c:c + 1], accum_out=rsum[:, c:c + 1])
                last.then_inc(s_exp, 1)

            def evac_qv(b):
                act.wait_ge(s_qvm, b.v + 1)
                if b.after(1):
                    act.wait_ge(s_s, b.v * NG)
                s.activation(qT[:].rearrange("p c n -> p (c n)"), bank_qv[0:DC, 0:2 * L], ACT.Copy,
                             scale=float(HS) ** -0.5).then_inc(s_qv, 1)
                if b.after(2):
                    act.wait_ge(s_pv, b.v - 1)
                s.activation(vs[:, b.parity, :, 0:HS], bank_qv[:, 2 * L:2 * L + D].rearrange(
                    "p (h d) -> p h d", h=NH), ACT.Copy).then_inc(s_qv, 1)

            def relu(b):
                act.wait_ge(s_ln, b.v * 7 + 4)
                if b.after(1):
                    act.wait_ge(s_h1b, b.v)
                s.activation(h1[:], un[:], ACT.Relu).then_inc(s_relu, 1)

            def evac_pt(b, k):
                act.wait_ge(s_ptm, b.v * NG + (k + 1))
                if b.after(1):
                    act.wait_ge(s_pv, b.v)
                s.activation(pT[:, HG * k:HG * (k + 1)].rearrange("p h n -> p (h n)"),
                             bank_s[k][:, 0:HG * L], ACT.Copy).then_inc(s_pt, 1)

            def evac_o(b):
                act.wait_ge(s_pv, b.v + 1)
                if b.after(1):
                    act.wait_ge(s_proj, b.v)
                s.activation(oT[:].rearrange("p h n -> p (h n)"), bank_o[:, 0:HG * L], ACT.Copy).then_inc(s_o, 1)

            def evac_t2(b):
                act.wait_ge(s_t2, b.v + 1)
                s.activation(xn2T[:, :, bass.ds(b.v * L, L)],
                             bank_k[0:DC, 0:2 * L].rearrange("p (c n) -> p c n", c=2), ACT.Copy).then_inc(s_xn2t, 1)

            def evac_t1(b):
                act.wait_ge(s_t1, b.v + 1)
                if b.after(1):
                    act.wait_ge(s_qvm, b.v)
                s.activation(xnT[0:DC].rearrange("p c n -> p (c n)"), bank_qv[0:DC, 0:2 * L],
                             ACT.Copy).then_inc(s_xnt, 1)

            def step(i):
                if i.inside():
                    for k in range(NG):
                        exp(i, k)
                if (i + 1).inside():
                    evac_qv(i + 1)
                if (i + 2).inside():
                    relu(i + 2)
                if i.inside():
                    for k in range(NG):
                        evac_pt(i, k)
                    evac_o(i)
                if (i + -1).inside():
                    evac_t2(i + -1)
                if (i + 2).inside():
                    evac_t1(i + 2)

            act.wait_ge(s_cd, 4)
            steps(act, step)

            for k in range(N // 512):
                act.wait_ge(s_lg, k + 1)
                s.activation(lgT[:, 512 * k:512 * (k + 1)], up_a[k % 2][0:NE, 0:512], ACT.Copy).then_inc(s_lgc, 1)
            act.wait_ge(s_rt, 2)
            s.activation(RT[1][:], RT[1][:], ACT.Exp).then_inc(s_rex, 1)

            def silu(u, u_par, n):
                act.wait_ge(s_u, u + 1)
                act.wait_ge(s_mul, u + 1)
                s.activation(sg[:, u_par, 0:n], up_a[u_par][:, 0:n], ACT.Silu).then_inc(s_silu, 1)

            with act.Fori(0, SH) as grp:
                for c in range(IC):
                    silu(grp * IC + c, c % 2, GN)

            def expert(e):
                for hf in range(2):
                    for c in range(IC):
                        silu(e.v * (2 * IC) + (U_E0 + hf * IC + c), c % 2, HALF)
                for t in range(CT):
                    act.wait_ge(s_d, e.v * CT + (D_E0 + t + 1))
                    s.activation(ys[:, bass.ds(e.v, 1), t, :].rearrange("p o d -> p (o d)"),
                                 down[(e.const * CT + t) % 2][:, 0:D], ACT.Copy).then_inc(s_ye, 1)

            act.wait_ge(s_zero, 16)
            with act.Fori(0, NE // 2 - 1) as r:
                expert(Tile(0, r))
                expert(Tile(1, r))
            expert(Tile(NE - 2))
            expert(Tile(NE - 1))
            for c in range(IC):
                silu(U_S3 + c, c % 2, GN)

        @block.tensor
        def _(pe):
            mm = nc.tensor.matmul

            def rows(c):
                return slice(0, DC + c)

            def pointwise(b):
                pe.wait_ge(s_conv, b.v * 14 + 14)
                if b.after(1):
                    pe.wait_ge(s_ln, b.v * 7 - 4)
                for c in range(2):
                    last = mm(bank_y[:, 0:D], cv[rows(c), b.parity, c], pw_sb[rows(c), c], start=c == 0, stop=c == 1)
                last.then_inc(s_y, 1)

            def turn_xn(b):
                pe.wait_ge(s_ln, b.v * 7 + 7)
                if b.after(1):
                    pe.wait_ge(s_qv, b.v * 2)
                for c in range(2):
                    last = nc.tensor.transpose(bank_qv[0:DC, c * L:(c + 1) * L], xn[:, c * DC:(c + 1) * DC], ident[:])
                last.then_inc(s_t1, 1)

            def qkv(b):
                pe.wait_ge(s_xnt, b.v + 1)
                if b.after(3):
                    pe.wait_ge(s_xn2t, b.v - 2)
                if b.after(1):
                    pe.wait_ge(s_kbd, b.v * 2)
                for m in range(2):
                    for c in range(2):
                        last = mm(bank_k[0:DC, m * L:(m + 1) * L], wqkv_sb[rows(c), c, D + m * DC:D + (m + 1) * DC],
                                  xnT[rows(c), c], start=c == 0, stop=c == 1)
                last.then_inc(s_k, 1)
                for m in range(2):
                    for c in range(2):
                        mm(bank_qv[0:DC, m * L:(m + 1) * L], wqkv_sb[rows(c), c, m * DC:(m + 1) * DC],
                           xnT[rows(c), c], start=c == 0, stop=c == 1)
                for c in range(2):
                    last = mm(bank_qv[:, 2 * L:2 * L + D], xnT[rows(c), c], wqkv_sb[rows(c), c, 2 * D:3 * D],
                              start=c == 0, stop=c == 1)
                last.then_inc(s_qvm, 1)

            def scores(b):
                pe.wait_ge(s_qv, b.v * 2 + 1)
                pe.wait_ge(s_kbd, b.v * 2 + 2)
                for k in range(NG):
                    if b.after(1):
                        pe.wait_ge(s_pt, b.v * NG + (k + 1 - NG))
                    m, h0 = k // 2, HG * (k % 2)
                    mm(bank_s[k][:, 0:HG * L], qT[:, m], kbd[:, m, h0:h0 + HG].rearrange("p h n -> p (h n)"),
                       start=True, stop=False)
                    mm(bank_s[k][:, 0:HG * L], identb[:], causal[:].rearrange("p h n -> p (h n)"),
                       start=False, stop=True).then_inc(s_s, 1)

            def turn_p(b):
                for k in range(NG):
                    pe.wait_ge(s_norm, b.v * NG + (k + 1))
                    for h in range(HG):
                        last = nc.tensor.transpose(bank_s[k][:, h * L:(h + 1) * L], probs[:, k, h], ident[:])
                    last.then_inc(s_ptm, 1)

            def pv(b):
                pe.wait_ge(s_qv, b.v * 2 + 2)
                pe.wait_ge(s_pt, b.v * NG + NG)
                if b.after(1):
                    pe.wait_ge(s_l3, b.v * 4 - 3)
                for h in range(NH):
                    j, q = h // 4, h % 4
                    last = mm(bank_o[32 * q:32 * q + 32, j * L:(j + 1) * L], vs[:, b.parity, h], pT[:, h],
                              start=True, stop=True)
                last.then_inc(s_pv, 1)

            def project(b):
                pe.wait_ge(s_o, b.v + 1)
                for j in range(HG):
                    last = mm(bank_o[:, 0:D], oT[:, j], wproj_sb[:, j], start=j == 0, stop=j == HG - 1)
                last.then_inc(s_proj, 1)

            def turn_xn2(b):
                pe.wait_ge(s_l3, b.v * 4 + 4)
                if b.reg is not None or b.const + 2 < NB:
                    pe.wait_ge(s_kbd, b.v * 2 + 6)
                if b.after(1):
                    pe.wait_ge(s_xn2t, b.v)
                for c in range(2):
                    last = nc.tensor.transpose(bank_k[0:DC, c * L:(c + 1) * L], xn2s[:, c * DC:(c + 1) * DC], ident[:])
                last.then_inc(s_t2, 1)

            def step(i):
                if i.inside():
                    scores(i)
                if (i + -1).inside():
                    project(i + -1)
                if (i + 1).inside():
                    qkv(i + 1)
                if i.inside():
                    turn_p(i)
                if (i + 3).inside():
                    pointwise(i + 3)
                if i.inside():
                    pv(i)
                if (i + -1).inside():
                    turn_xn2(i + -1)
                if (i + 2).inside():
                    turn_xn(i + 2)

            pe.wait_ge(s_cst, 1)
            pe.wait_ge(s_cd, 4)
            pe.wait_ge(s_wa, 16 * N_WA)
            steps(pe, step)

            pe.wait_ge(s_sw, 16 * 4)
            pe.wait_ge(s_xn2t, NB)
            for k in range(N // 512):
                if k >= 2:
                    pe.wait_ge(s_lgc, k - 1)
                for c in range(2):
                    last = mm(up_a[k % 2][0:NE, 0:512], wr_sb[:, c], xn2T[:, c, 512 * k:512 * (k + 1)],
                              start=c == 0, stop=c == 1)
                last.then_inc(s_lg, 1)
            pe.wait_ge(s_lgc, N // 512)
            for t in range(NB):
                last = nc.tensor.transpose(turn[0][:, t * NE:(t + 1) * NE], lgT[:, t * L:(t + 1) * L], ident[0:NE, 0:NE])
            last.then_inc(s_lgt, 1)

            def up(u, par, w_a, w_b, rhs, n):
                pe.wait_ge(s_mul, u + 1)
                for bank, w in ((up_a, w_a), (up_b, w_b)):
                    for c in range(2):
                        last = mm(bank[par][:, 0:n], w(c), rhs(c), start=c == 0, stop=c == 1)
                last.then_inc(s_u, 1)

            def down_tile(d, par, u_done, c0, w):
                pe.wait_ge(s_mul, u_done + FREE)
                pe.wait_ge(s_ye, d + 1)
                for c in range(IC):
                    last = mm(down[par][:, 0:D], G[:, c, c0:c0 + 128], w(c), start=c == 0, stop=c == IC - 1)
                last.then_inc(s_d, 1)

            def shared(grp, u0, d0, between=None):
                for c in range(IC):
                    cs = slice(c * 128, (c + 1) * 128)
                    up(u0 + c, c % 2, lambda k: S1[:, k, cs], lambda k: S3[:, k, cs],
                       lambda k: xn2T[:, k, bass.ds(grp * GN, GN)], GN)
                for t in range(GT):
                    down_tile(d0 + t, t % 2, u0 + IC, t * 128, lambda k: S2[:, k])

            with pe.Fori(0, SH) as grp:
                shared(grp, grp * IC, grp * GT)

            for n in range(2):
                pe.wait_ge(s_pre, 2 * n + 1)
                m = RT[4 + n]
                mm(turn[1][:, 0:NB * NE], tri[:], m[:].rearrange("p t e -> p (t e)"), start=True, stop=True)
                mm(turn[1][:, 128:128 + NB * NE], ones[:], m[:].rearrange("p t e -> p (t e)"),
                   start=True, stop=True).then_inc(s_lgt, 1)

            def turn_slots(e, t):
                if t == 0:
                    pe.wait_ge(s_xg[e.parity], e.pair * 16 + 16)
                if e.reg is not None or e.const * CT + t >= 2:
                    pe.wait_ge(s_xte, e.v * CT + (t - 1))
                for c in range(2):
                    last = nc.tensor.transpose(turn[(e.const * CT + t) % 2][0:DC, c * 128:(c + 1) * 128],
                                               xg[:, e.parity, t, c * DC:(c + 1) * DC], ident[:])
                last.then_inc(s_xt, 1)

            def expert(e, more):
                p = e.parity
                pe.wait_ge(s_w[p], e.pair * 48 + 48)
                pe.wait_ge(s_xte, e.v * CT + CT)
                for hf in range(2):
                    for c in range(IC):
                        cs = slice(c * 128, (c + 1) * 128)
                        up(e.v * (2 * IC) + (U_E0 + hf * IC + c), c % 2,
                           lambda k: W1[:, p, k, cs], lambda k: W3[:, p, k, cs],
                           lambda k: xgT[:, p, k, hf * HALF:(hf + 1) * HALF], HALF)
                        if hf == 1 and c < CT and more:
                            turn_slots(e + 1, c)
                for t in range(CT):
                    u_done = U_E0 + (IC if (t + 1) * 128 <= HALF else 2 * IC)
                    down_tile(e.v * CT + (D_E0 + t), (e.const * CT + t) % 2, e.v * (2 * IC) + u_done, t * 128,
                              lambda k: W2[:, p, k])

            for t in range(CT):
                turn_slots(Tile(0), t)
            with pe.Fori(0, NE // 2 - 1) as r:
                expert(Tile(0, r), True)
                expert(Tile(1, r), True)
            expert(Tile(NE - 2), True)
            expert(Tile(NE - 1), False)
            shared(SH, U_S3, D_S3)

        @block.vector
        def _(dve):
            v = nc.vector
            v.memset(cv[DC:DC + 1, :, 1, :], 1.0).then_inc(s_cd, 1)
            v.memset(xnT[DC:DC + 1, 1, :], 1.0).then_inc(s_cd, 1)
            v.memset(vs[:], 0.0).then_inc(s_cd, 1)
            v.memset(ys[:].rearrange("p e t d -> p (e t d)"), 0.0).then_inc(s_zf, 1)
            v.memset(thr[:], 0).then_inc(s_cd, 1)
            v.memset(bit[:], 1 << (BITS - 1)).then_inc(s_cd, 1)
            dve.wait_ge(s_cst, 1)
            dve.wait_ge(s_wa, 16 * N_WA)
            dve.wait_ge(s_bc, 16 * 3)
            dve.sem_inc(s_mul, FREE)
            dve.sem_inc(s_ye, FREE)

            def conv(b, part):
                taps = [range(0, 2), range(2, 4), range(4, 6), range(6, 7)][part]
                if part == 0:
                    dve.wait_ge(s_x[b.parity], b.pair * 16 + 16)
                    if b.after(2):
                        dve.wait_ge(s_y, b.v - 1)
                for k in taps:
                    for c in range(2):
                        acc, src = cv[0:DC, b.parity, c], xb[:, b.parity, c, k:k + L]
                        if k == 0:
                            v.tensor_scalar(acc, src, dw_sb[:, c, k:k + 1], None, ALU.mult).then_inc(s_conv, 1)
                        else:
                            dve.wait_ge(s_conv, b.v * 14 + (2 * k + c - 1))
                            v.scalar_tensor_tensor(acc, src, dw_sb[:, c, k:k + 1], acc, ALU.mult,
                                                   ALU.add).then_inc(s_conv, 1)

            def maxima(b, k):
                dve.wait_ge(s_s, b.v * NG + (k + 1))
                v.tensor_reduce(nmax[:, HG * k:HG * (k + 1)], bank_s[k][:, 0:HG * L].rearrange(
                    "p (h n) -> p h n", h=HG), AX.X, ALU.max, negate=True).then_inc(s_max, 1)

            def inverse(b, k):
                dve.wait_ge(s_exp, b.v * NG + (k + 1))
                if b.after(1):
                    dve.wait_ge(s_norm, b.v * NG + (k + 1 - NG))
                v.reciprocal(rinv[:, HG * k:HG * (k + 1)], rsum[:, HG * k:HG * (k + 1)]).then_inc(s_rinv, 1)

            def keys(b):
                dve.wait_ge(s_k, b.v + 1)
                if b.after(1):
                    dve.wait_ge(s_s, b.v * NG)
                for m in range(2):
                    v.tensor_tensor(kbd[:, m], bank_k[0:DC, m * L:(m + 1) * L].unsqueeze(1).to_broadcast([DC, 6, L]),
                                    headmask[:].unsqueeze(2).to_broadcast([DC, 6, L]), ALU.mult).then_inc(s_kbd, 1)

            def ln1_stats(b):
                dve.wait_ge(s_y, b.v + 1)
                v.bn_stats(st[:, 0], bank_y[:, 0:D]).then_inc(s_ln, 1)
                dve.wait_ge(s_ln, b.v * 7 + 1)
                if b.after(1):
                    dve.wait_ge(s_r1, b.v * 2)
                v.memset(carry[:, 0:1], 0.0)
                v.bn_aggr(mv[:, 0], st[:, 0]).then_inc(s_ln, 1)
                dve.wait_ge(s_ln, b.v * 7 + 2)

            def ln1_apply(b):
                v.scalar_tensor_tensor(tn[:], bank_y[:, 0:D], mv[:, 0, 0:1], g_bc[:], ALU.subtract,
                                       ALU.mult).then_inc(s_ln, 1)
                dve.wait_ge(s_ln, b.v * 7 + 3)
                dve.wait_ge(s_r1, b.v * 2 + 2)
                if b.after(1):
                    dve.wait_ge(s_relu, b.v)
                v.scalar_tensor_tensor(un[:], tn[:], rstd[:, 0], b_bc[:], ALU.mult, ALU.add).then_inc(s_ln, 1)

            def ln2_stats(b):
                dve.wait_ge(s_relu, b.v + 1)
                v.bn_stats(st[:, 1], h1[:]).then_inc(s_ln, 1)
                dve.wait_ge(s_ln, b.v * 7 + 5)
                if b.after(1):
                    dve.wait_ge(s_r2, b.v * 2)
                v.memset(carry[:, 1:2], 0.0)
                v.bn_aggr(mv[:, 1], st[:, 1]).then_inc(s_ln, 1)
                dve.wait_ge(s_ln, b.v * 7 + 6)

            def ln2_apply(b):
                dve.wait_ge(s_r2, b.v * 2 + 2)
                if b.after(1):
                    dve.wait_ge(s_t1, b.v)
                v.tensor_scalar(xn[:], h1[:], mv[:, 1, 0:1], rstd[:, 1], ALU.subtract, ALU.mult).then_inc(s_ln, 1)

            def ln3(b):
                row = H[:, bass.ds(b.v, 1)].rearrange("p o d -> p (o d)")
                dve.wait_ge(s_proj, b.v + 1)
                dve.wait_ge(s_h1b, b.v + 1)
                if b.after(1):
                    dve.wait_ge(s_xc, b.v * 2)
                v.tensor_tensor(hrow[:], bank_o[:, 0:D], row, ALU.add).then_inc(s_l3, 1)
                dve.wait_ge(s_l3, b.v * 4 + 1)
                v.bn_stats(st[:, 2], hrow[:]).then_inc(s_l3, 1)
                dve.wait_ge(s_l3, b.v * 4 + 2)
                v.memset(carry[:, 2:3], 0.0)
                v.bn_aggr(mv[:, 2], st[:, 2]).then_inc(s_l3, 1)
                dve.wait_ge(s_l3, b.v * 4 + 3)
                dve.wait_ge(s_r3, b.v * 2 + 2)
                if b.after(1):
                    dve.wait_ge(s_t2, b.v)
                v.tensor_scalar(xn2s[:], hrow[:], mv[:, 2, 0:1], rstd[:, 2], ALU.subtract, ALU.mult).then_inc(s_l3, 1)

            def step(i):
                a, n, x, m = i, i + 2, i + 4, i + -1
                if a.inside():
                    for k in range(NG):
                        maxima(a, k)
                if x.inside():
                    conv(x, 0)
                if a.inside():
                    inverse(a, 0)
                if n.inside():
                    ln1_stats(n)
                if a.inside():
                    inverse(a, 1)
                if (i + 1).inside():
                    keys(i + 1)
                if n.inside():
                    ln1_apply(n)
                if a.inside():
                    inverse(a, 2)
                if x.inside():
                    conv(x, 1)
                if a.inside():
                    inverse(a, 3)
                if n.inside():
                    ln2_stats(n)
                if x.inside():
                    conv(x, 2)
                if n.inside():
                    ln2_apply(n)
                if m.inside():
                    ln3(m)
                if x.inside():
                    conv(x, 3)

            steps(dve, step)

            chain = [0]

            def link(ins, k=1):
                chain[0] += 1
                ins.then_inc(s_rt, 1)
                dve.wait_ge(s_rt, chain[0])

            def wide(ap):
                return ap.unsqueeze(2).to_broadcast([128, NB, NE])

            dve.wait_ge(s_lgt, 1)
            lg = turn[0][:, 0:NB * NE].rearrange("p (t e) -> p t e", e=NE)
            link(v.tensor_reduce(RS[0][:], lg, AX.X, ALU.max))
            link(v.tensor_tensor(RT[1][:], lg, wide(RS[0][:]), ALU.subtract))
            dve.wait_ge(s_rex, 1)
            link(v.tensor_reduce(RS[1][:], RT[1][:], AX.X, ALU.add))
            link(v.reciprocal(RS[2][:], RS[1][:]))
            link(v.tensor_tensor(RT[0][:], RT[1][:], wide(RS[2][:]), ALU.mult))

            def best(j):
                link(v.tensor_reduce(RS[j][:], RT[0][:], AX.X, ALU.max))
                link(v.tensor_tensor(RT[1][:], RT[0][:], wide(RS[j][:]), ALU.is_equal))
                link(v.tensor_tensor(RT[1][:], RT[1][:], edesc[:], ALU.mult))
                link(v.tensor_reduce(RS[2][:], RT[1][:], AX.X, ALU.max))
                link(v.tensor_tensor(oh[:, j], edesc[:], wide(RS[2][:]), ALU.is_equal))

            best(0)
            link(v.scalar_tensor_tensor(RT[0][:].rearrange("p t e -> p (t e)"),
                                        oh[:, 0].rearrange("p t e -> p (t e)"), -2.0,
                                        RT[0][:].rearrange("p t e -> p (t e)"), ALU.mult, ALU.add))
            best(1)
            link(v.tensor_tensor(RS[2][:], RS[0][:], RS[1][:], ALU.add))
            link(v.tensor_scalar(RS[2][:], RS[2][:], 1e-9, None, ALU.max))
            link(v.reciprocal(RS[3][:], RS[2][:]))
            for j in range(2):
                link(v.tensor_tensor(wgt[:, j], RS[j][:], RS[3][:], ALU.mult))
                link(v.tensor_tensor(RT[1 + j][:], oh[:, j], wide(wgt[:, j]), ALU.mult))
            link(v.tensor_tensor(RT[3][:], oh[:, 0], oh[:, 1], ALU.add))
            link(v.tensor_tensor(RT[1][:], RT[1][:], RT[2][:], ALU.add))
            link(v.scalar_tensor_tensor(score[:].rearrange("p t e -> p (t e)"),
                                        RT[3][:].rearrange("p t e -> p (t e)"), 1.0,
                                        RT[1][:].rearrange("p t e -> p (t e)"), ALU.subtract, ALU.add))

            def over(ap):
                return ap.unsqueeze(1).to_broadcast([128, NB, NE])

            def search():
                k = len(searched)
                searched.append(k)
                w = 7 * k
                v.tensor_tensor(cand[:], thr[:], bit[:], ALU.bitwise_or).then_inc(s_thr, 1)
                dve.wait_ge(s_thr, w + 1)
                v.tensor_tensor(RT[6][:], score[:], over(cand[:].bitcast(F32)), ALU.is_ge).then_inc(s_thr, 1)
                v.tensor_scalar(bit[:], bit[:], 1, None, ALU.logical_shift_right).then_inc(s_thr, 1)
                dve.wait_ge(s_thr, w + 3)
                v.tensor_reduce(cnt[:], RT[6][:].rearrange("p t e -> p e t"), AX.X, ALU.add).then_inc(s_cnt, 1)
                dve.wait_ge(s_tot, k + 1)
                v.tensor_scalar(ge[:], tot[:], float(CAP), None, ALU.is_ge).then_inc(s_thr, 1)
                dve.wait_ge(s_thr, w + 4)
                v.copy_predicated(thr[:], ge[:], cand[:]).then_inc(s_thr, 3)
                dve.wait_ge(s_thr, w + 7)

            searched = []

            def gated(u, par, c, c0, n):
                dve.wait_ge(s_silu, u + 1)
                v.tensor_tensor(G[:, c, c0:c0 + n], sg[:, par, 0:n], up_b[par][:, 0:n], ALU.mult).then_inc(s_mul, 1)

            def add_shared(d, par, tile):
                dve.wait_ge(s_d, d + 1)
                row = H[:, bass.ds(tile, 1)].rearrange("p o d -> p (o d)")
                v.tensor_tensor(row, down[par][:, 0:D], row, ALU.add).then_inc(s_ye, 1)

            def masks():
                t = thr[:].bitcast(F32)
                link(v.tensor_tensor(RT[3][:], score[:], over(t), ALU.is_gt))
                link(v.tensor_reduce(cnt[:], RT[3][:].rearrange("p t e -> p e t"), AX.X, ALU.add))
                v.sem_inc(s_cnt, 1)
                v.tensor_tensor(RT[4][:], score[:], over(t), ALU.is_equal).then_inc(s_pre, 1)

            def ranks(n, mask, res):
                dve.wait_ge(s_lgt, 2 + n)
                by_e = "p t e -> p e t"
                all_p = turn[1][:, 128:128 + NB * NE].rearrange("p (t e) -> p e t", e=NE)
                tr = RT[6][:].rearrange("p t e -> p (t e)").rearrange("p (e t) -> p e t", e=NE)
                flat = "p e t -> p (e t)"
                link(v.tensor_copy(tr, all_p))
                sc = RT[7][:].rearrange("p t e -> p (t e)")
                link(v.tensor_tensor_scan(sc, segm[:].rearrange(flat), tr.rearrange(flat), 0.0, ALU.mult, ALU.add))
                link(v.tensor_tensor(sc, sc, tr.rearrange(flat), ALU.subtract))
                link(v.tensor_tensor(res, turn[1][:, 0:NB * NE].rearrange("p (t e) -> p t e", e=NE),
                                     sc.rearrange("p (e t) -> p t e", e=NE), ALU.add))

            def place():
                ranks(0, RT[4], RT[1][:])
                dve.wait_ge(s_tot, BITS + 1)
                link(v.tensor_tensor(RT[1][:], RT[1][:], over(tot[:]), ALU.add))
                link(v.tensor_scalar(RT[1][:], RT[1][:], float(CAP), None, ALU.is_lt))
                link(v.tensor_tensor(RT[1][:], RT[1][:], RT[4][:], ALU.mult))
                link(v.tensor_tensor(RT[5][:], RT[1][:], RT[3][:], ALU.add))
                v.sem_inc(s_pre, 2)
                ranks(1, RT[5], RT[1][:])
                link(v.tensor_tensor(RT[1][:], RT[1][:], ebase[:], ALU.add))
                for j in range(2):
                    link(v.tensor_tensor(RT[2][:], oh[:, j], RT[1][:], ALU.mult))
                    link(v.tensor_reduce(RS[0][:], RT[2][:], AX.X, ALU.add))
                    link(v.tensor_tensor(RT[2][:], oh[:, j], RT[5][:], ALU.mult))
                    link(v.tensor_reduce(RS[1][:], RT[2][:], AX.X, ALU.add))
                    link(v.tensor_tensor(wgt[:, j], wgt[:, j], RS[1][:], ALU.mult))
                    link(v.tensor_tensor(src_i[:, j], RS[0][:], RS[1][:], ALU.mult))
                    link(v.tensor_tensor(RS[0][:], RS[0][:], dump[:, j], ALU.subtract))
                    link(v.tensor_tensor(RS[0][:], RS[0][:], RS[1][:], ALU.mult))
                    link(v.tensor_tensor(dst_i[:, j], RS[0][:], dump[:, j], ALU.add))
                v.sem_inc(s_ix, 1)

            for grp in range(SH):
                for c in range(IC):
                    gated(grp * IC + c, c % 2, c, 0, GN)
                    for _ in range([3, 2][(grp * IC + c) % 2] if len(searched) < BITS else 0):
                        search()
                for t in range(GT):
                    add_shared(grp * GT + t, t % 2, grp * GT + t)
            masks()
            place()

            def turned(e, t):
                dve.wait_ge(s_xt, e.v * CT + (t + 1))
                v.tensor_copy(xgT[:, e.parity, :, t * 128:(t + 1) * 128],
                              turn[(e.const * CT + t) % 2][0:DC, 0:256].rearrange(
                                  "p (c n) -> p c n", c=2)).then_inc(s_xte, 1)

            def expert(e, more):
                for hf in range(2):
                    for c in range(IC):
                        gated(e.v * (2 * IC) + (U_E0 + hf * IC + c), c % 2, c, hf * HALF, HALF)
                        if hf == 1 and c < CT and more:
                            turned(e + 1, c)

            for t in range(CT):
                turned(Tile(0), t)
            with dve.Fori(0, NE // 2 - 1) as r:
                expert(Tile(0, r), True)
                expert(Tile(1, r), True)
            expert(Tile(NE - 2), True)
            expert(Tile(NE - 1), False)
            for c in range(IC):
                gated(U_S3 + c, c % 2, c, 0, GN)
            for t in range(GT):
                add_shared(D_S3 + t, t % 2, SH * GT + t)

            for t in range(NB):
                dve.wait_ge(s_g[t % 4], 32 * (t // 4 + 1))
                for j in range(2):
                    v.scalar_tensor_tensor(H[:, t, :], gath[:, t % 4, j], wgt[:, j, t:t + 1], H[:, t, :],
                                           ALU.mult, ALU.add).then_inc(s_cmb, 1)
                    dve.wait_ge(s_cmb, 2 * t + j + 1)


_OUT = (NB, L, D)


def kernel(x, L0_tok_dw_w, L0_tok_pw_w, L0_tok_pw_b, L0_tok_ln_g, L0_tok_ln_b, L0_attn_W_attn,
           L0_attn_b_attn, L0_attn_W_proj, L0_attn_b_proj, L0_ffn_Wr, L0_ffn_w1, L0_ffn_w3, L0_ffn_w2,
           L0_ffn_s1, L0_ffn_s3, L0_ffn_s2):
    import numpy as np
    import concourse.bacc as bacc
    from concourse.bass_utils import run_bass_kernel_spmd

    def chunks(w):
        w = np.asarray(w)
        return np.ascontiguousarray(np.moveaxis(w.reshape(w.shape[:-2] + (2, DC, w.shape[-1])), -3, -2))

    def inner(w):
        w = np.asarray(w)
        return np.ascontiguousarray(np.moveaxis(w.reshape(w.shape[:-2] + (IC, 128, w.shape[-1])), -3, -2))

    x = np.asarray(x)[..., 0]
    pad = (TAPS - 1) // 2
    xp = np.zeros((NB, L + 2 * pad, D), x.dtype)
    xp[:, pad:pad + L] = x
    wp = np.zeros((4, HG, 32, D), x.dtype)
    wp[:, :, 0:HS] = np.asarray(L0_attn_W_proj).reshape(HG, 4, HS, D).transpose(1, 0, 2, 3)
    arrays = {
        "xT": np.ascontiguousarray(xp.transpose(2, 0, 1).reshape(2, DC, NB, L + 2 * pad).transpose(1, 0, 2, 3)),
        "dw": chunks(np.asarray(L0_tok_dw_w).reshape(D, TAPS)),
        "pwT": chunks(np.asarray(L0_tok_pw_w).T),
        "pw_b": np.asarray(L0_tok_pw_b).reshape(1, D),
        "ln_g": np.asarray(L0_tok_ln_g),
        "ln_b": np.asarray(L0_tok_ln_b),
        "wqkv": chunks(L0_attn_W_attn),
        "b_attn": np.asarray(L0_attn_b_attn).reshape(1, 3 * D),
        "wproj": np.ascontiguousarray(wp.transpose(0, 2, 1, 3).reshape(128, HG, D)),
        "b_proj": np.asarray(L0_attn_b_proj),
        "wr": chunks(L0_ffn_Wr),
        "w1": chunks(L0_ffn_w1), "w3": chunks(L0_ffn_w3), "w2": inner(L0_ffn_w2),
        "s1": chunks(L0_ffn_s1), "s3": chunks(L0_ffn_s3), "s2": inner(L0_ffn_s2),
    }
    nc = bacc.Bacc("TRN2", target_bir_lowering=False, num_devices=1)
    ins = [nc.dram_tensor(n, a.shape, mybir.dt.from_np(a.dtype), kind="ExternalInput").ap() for n, a in arrays.items()]
    out = nc.dram_tensor("out", _OUT, F32, kind="ExternalOutput").ap()
    vit_tower(nc, *ins, out)
    r = run_bass_kernel_spmd(nc, [arrays], core_ids=[0])
    return r.results[0]["out"]
```

```python
from contextlib import ExitStack

import concourse.bass as bass
from concourse import mybir

ALU = mybir.AluOpType
ACT = mybir.ActivationFunctionType
AX = mybir.AxisListType
F32 = mybir.dt.float32
F32R = mybir.dt.float32r
BF16 = mybir.dt.bfloat16
I32 = mybir.dt.int32
RADD = bass.bass_isa.ReduceOp.add

NB, L, D = 16, 128, 192
N = NB * L
DC = 96
DA, DB = 128, D - 128
DW = D + DB
HI_A, HI_LO_B, LO_A = range(3)
TAPS = 7
NH, HS = 12, 16
HG = 3
NG = NH // HG
NE, INNER = 8, 768
IC = INNER // 128
RW = DW + NE + 1
CAP = (N * 2 * 5 // 4) // NE
CT = CAP // 128
HALF = CAP // 2
GT = 4
GN = GT * L
NEG = -1.0e30
ACTIVE = range(-4, NB + 2)
FIRST, LAST = 2, 11
BITS = 30


class Tile:

    def __init__(self, const, reg=None):
        self.const, self.reg = const, reg

    def __add__(self, k):
        return Tile(self.const + k, self.reg)

    @property
    def v(self):
        return self.const if self.reg is None else self.reg * 2 + self.const

    @property
    def pair(self):
        return self.const // 2 if self.reg is None else self.reg + self.const // 2

    @property
    def parity(self):
        return self.const % 2

    def inside(self):
        return self.reg is not None or 0 <= self.const < NB

    def after(self, k):
        return self.reg is not None or self.const >= k


def vit_tower(nc, xT, dw, pwT, pw_b, ln_g, ln_b, wqkv, b_attn, wproj, b_proj, wr, w13, w2,
              s13, s2, out):
    with ExitStack() as ctx:
        def sb(name, shape, dt=F32, scope=ctx):
            return scope.enter_context(nc.sbuf_tensor(name, shape, dt))

        def ps(name, shape, dt=F32):
            return ctx.enter_context(nc.psum_tensor(name, shape, dt))

        def sem(name):
            return ctx.enter_context(nc.semaphore(name))

        slots_in = nc.dram_tensor("slots_in", [NE * CAP + 2 * N, RW], F32).ap()
        acc = nc.dram_tensor("acc", [1 + N + 2 * CAP, D], F32).ap()

        wr_raw = sb("wr_raw", [128, 2, NE])
        wr_sp = sb("wr_sp", [128, 4, 128], F32R)
        ident = sb("ident", [128, 128])
        tri = sb("tri", [128, 128])
        ones = sb("ones", [128, 128])
        H = sb("H", [128, NB, D])
        xn2 = sb("xn2", [128, NB, RW])
        xs = sb("xs", [128, 3, N], F32R)
        edesc = sb("edesc", [128, NB, NE])
        ebase = sb("ebase", [128, NB, NE])
        dump = sb("dump", [128, 2, NB])
        rt = sb("rt", [128, 8, NB, NE])
        RT = [rt[:, i] for i in range(8)]
        RS = [sb(f"rs{i}", [128, NB]) for i in range(4)]
        score = sb("score", [128, NB, NE])
        oh = sb("oh", [128, 2, NB, NE])
        wgt = sb("wgt", [128, 2, NB])
        thr = sb("thr", [128, NE], I32)
        digit = sb("digit", [128, 3, NE], I32)
        cand = sb("cand", [128, 3, NE], I32)
        above = rt[:, 3:6]
        cnt = sb("cnt", [128, 3, NE])
        tot = sb("tot", [128, 3, NE])
        ge = sb("ge", [128, 3, NE], I32)
        dst_i = sb("dst_i", [128, 2, NB], I32)
        spare = sb("spare", [128, 2, CT])
        unused = sb("unused", [128, CT])
        wslot = sb("wslot", [128, 2, CT])
        row_i = sb("row_i", [128, 2, CT], I32)
        segm = sb("segm", [128, NE, NB])
        raw_a = sb("raw_a", [128, 2, INNER])
        raw_b = sb("raw_b", [128, 2, INNER])
        raw_2 = sb("raw_2", [128, IC, D])
        wa = sb("wa", [128, 2, 2, 2, INNER], F32R)
        wb_hi = sb("wb_hi", [128, 2, 2, INNER], F32R)
        wb_lo = sb("wb_lo", [DB, 2, 2, INNER], F32R)
        w2s = sb("w2s", [128, 2, IC, 2, D], F32R)
        ctx_a = ExitStack()

        def sa(name, shape, dt=F32):
            return sb(name, shape, dt, ctx_a)

        xb = sa("xb", [DC, 2, 2, L + TAPS - 1])
        dw_sb = sa("dw_sb", [DC, 2, TAPS])
        cv = sa("cv", [DC + 1, 2, 2, L])
        pw_sb = sa("pw_sb", [DC + 1, 2, D])
        g_bc = sa("g_bc", [128, D])
        b_bc = sa("b_bc", [128, D])
        bproj_bc = sa("bproj_bc", [128, D])
        wqkv_sb = sa("wqkv_sb", [DC + 1, 2, 3 * D])
        wproj_sb = sa("wproj_sb", [128, HG, D])
        identb = sa("identb", [128, 128], BF16)
        causal = sa("causal", [128, HG, L], BF16)
        headmask = sa("headmask", [DC, 6])
        eps1 = sa("eps1", [128, 1])
        eps2 = sa("eps2", [128, 1])
        mhalf = sa("mhalf", [128, 1])
        st = sa("st", [128, 3, 6])
        mv = sa("mv", [128, 3, 2])
        ve = sa("ve", [128, 3, 1])
        rstd = sa("rstd", [128, 3, 1])
        carry = sa("carry", [128, 3])
        tn = sa("tn", [128, D])
        un = sa("un", [128, D])
        h1 = sa("h1", [128, D])
        xn = sa("xn", [128, D])
        xnT = sa("xnT", [DC + 1, 2, L])
        qT = sa("qT", [DC, 2, L])
        kbd = sa("kbd", [DC, 2, 6, L])
        vs = sa("vs", [128, 2, NH, 32])
        probs = sa("probs", [128, NG, HG, L])
        nmax = sa("nmax", [128, NH])
        rsum = sa("rsum", [128, NH])
        rinv = sa("rinv", [128, NH])
        pT = sa("pT", [128, NH, L])
        oT = sa("oT", [128, HG, L])
        hrow = sa("hrow", [128, D])
        xn2s = sa("xn2s", [128, DW])
        ctx_a.close()
        sgf = sb("sgf", [128, 2, 2, GN])
        sg, gf = sgf[:, 0], sgf[:, 1]
        lgT = sgf[0:NE].rearrange("p a b n -> p (a b n)")
        G = sb("G", [128, 2, IC, CAP], F32R)
        xgs = sb("xgs", [128, 2, 3, CAP], F32R)
        ys = sb("ys", [128, 2, CT, D])
        flat_xn2 = xn2[:].rearrange("p t d -> p (t d)")
        xg = flat_xn2[:, 0:2 * CT * RW].rearrange("p (q t d) -> p q t d", q=2, t=CT)

        bank_qv = ps("bank_qv", [128, 512])
        bank_k = ps("bank_k", [128, 512])
        bank_s = [ps(f"bank_s{g}", [128, 512]) for g in range(NG)]
        bank_o = ps("bank_o", [128, 512])
        bank_y = ps("bank_y", [128, 512])
        up_a, up_b = bank_s[0:2], bank_s[2:4]
        down = [bank_o, bank_y]
        turn = [bank_qv, bank_k]

        s_x = [sem("s_x0"), sem("s_x1")]
        s_wa = sem("s_wa")
        s_bc = sem("s_bc")
        s_cst = sem("s_cst")
        s_cd = sem("s_cd")
        s_pc = sem("s_pc")
        s_conv = sem("s_conv")
        s_y = sem("s_y")
        s_ln = sem("s_ln")
        s_r1 = sem("s_r1")
        s_r2 = sem("s_r2")
        s_r3 = sem("s_r3")
        s_relu = sem("s_relu")
        s_h1b = sem("s_h1b")
        s_t1 = sem("s_t1")
        s_xnt = sem("s_xnt")
        s_k = sem("s_k")
        s_qvm = sem("s_qvm")
        s_qv = sem("s_qv")
        s_kbd = sem("s_kbd")
        s_s = sem("s_s")
        s_max = sem("s_max")
        s_exp = sem("s_exp")
        s_rinv = sem("s_rinv")
        s_norm = sem("s_norm")
        s_ptm = sem("s_ptm")
        s_pt = sem("s_pt")
        s_pv = sem("s_pv")
        s_o = sem("s_o")
        s_proj = sem("s_proj")
        s_l3 = sem("s_l3")
        s_t2 = sem("s_t2")
        s_xn2t = sem("s_xn2t")
        s_xlo = sem("s_xlo")
        s_raw = [sem(f"s_raw{i}") for i in range(3)]
        s_hiw = sem("s_hiw")
        s_low = sem("s_low")
        s_hi = sem("s_hi")
        s_lo = sem("s_lo")
        s_hc = sem("s_hc")
        s_wrs = sem("s_wrs")
        s_zero = sem("s_zero")
        s_zf = sem("s_zf")
        s_lg = sem("s_lg")
        s_lgc = sem("s_lgc")
        s_lgt = sem("s_lgt")
        s_rt = sem("s_rt")
        s_rex = sem("s_rex")
        s_thr = sem("s_thr")
        s_cnt = sem("s_cnt")
        s_tot = sem("s_tot")
        s_pre = sem("s_pre")
        s_ix = sem("s_ix")
        s_scat = sem("s_scat")
        s_sw = sem("s_sw")
        s_xg = [sem("s_xg0"), sem("s_xg1")]
        s_u = sem("s_u")
        s_silu = sem("s_silu")
        s_mul = sem("s_mul")
        s_d = sem("s_d")
        s_ye = sem("s_ye")
        s_xt = sem("s_xt")
        s_xte = sem("s_xte")
        s_xhi = sem("s_xhi")
        s_add = [sem("s_add0"), sem("s_add1")]
        s_info = sem("s_info")
        s_sh = sem("s_sh")
        s_y1 = sem("s_y1")
        s_unused = sem("s_unused")
        s_wt = sem("s_wt")
        s_base = sem("s_base")
        s_out = sem("s_out")

        N_ZERO = -(-NE * CAP * RW // 128 // (2 * CT * D))
        N_WA = 6
        FREE = 2
        ADDED = 16 * CT
        SH = NB // GT
        POOL_LO = 2
        HI_AT = 3
        PIECES = 11
        EARLY = 3
        U_E0, D_E0 = SH * IC, SH * GT

        def search_at(grp, chunk=None, tile=None):
            if grp == 0:
                return tile is not None or chunk >= 2
            return grp == 1 and (chunk is not None or tile == 0)

        def steps(eng, body):
            for i in ACTIVE:
                if i < FIRST or i > LAST:
                    body(Tile(i))
                elif i == FIRST:
                    with eng.Fori(0, (LAST - FIRST + 1) // 2) as r:
                        body(Tile(FIRST, r))
                        body(Tile(FIRST + 1, r))

        block = ctx.enter_context(nc.Block())

        @block.sync
        def _(sp):
            def load_x(b):
                if b.after(2):
                    sp.wait_ge(s_conv, b.v * 14 - 14)
                sp.dma_start(xb[:, b.parity, :, :], xT[:, :, bass.ds(b.v, 1), :].rearrange(
                    "p c o n -> p c (o n)")).then_inc(s_x[b.parity], 16)

            load_x(Tile(0))
            sp.dma_start(dw_sb[:], dw).then_inc(s_wa, 16)
            load_x(Tile(1))
            sp.dma_start(pw_sb[0:DC], pwT).then_inc(s_wa, 16)
            sp.dma_start(pw_sb[DC:DC + 1, 1, :], pw_b).then_inc(s_wa, 16)
            sp.dma_start(g_bc[:], ln_g.partition_broadcast(128)).then_inc(s_bc, 16)
            sp.dma_start(b_bc[:], ln_b.partition_broadcast(128)).then_inc(s_bc, 16)
            sp.dma_start(wqkv_sb[0:DC], wqkv).then_inc(s_wa, 16)
            sp.dma_start(wqkv_sb[DC:DC + 1, 1, :], b_attn).then_inc(s_wa, 16)
            sp.dma_start(bproj_bc[:], b_proj.partition_broadcast(128)).then_inc(s_bc, 16)
            sp.dma_start(wproj_sb[:], wproj).then_inc(s_wa, 16)
            sp.dma_start(wr_raw[:, 0], wr[0:DA]).then_inc(s_sw, 16)
            for half in (wr_raw[0:DB, 1], wr_raw[DB:128, 1]):
                sp.dma_start(half, wr[DA:D]).then_inc(s_sw, 16)

            def load_w(gate_up, w_down, hi=None, low=None):
                if low is not None:
                    sp.wait_ge(s_hiw, hi)
                    sp.wait_ge(s_low, low(4))
                sp.dma_start(raw_a[:], gate_up[0:DA]).then_inc(s_raw[0], 16)
                if low is not None:
                    sp.wait_ge(s_low, low(8))
                sp.dma_start(raw_b[0:DB], gate_up[DA:D]).then_inc(s_raw[1], 16)
                sp.dma_start(raw_b[DB:128], gate_up[DA:D]).then_inc(s_raw[1], 16)
                if low is not None:
                    sp.wait_ge(s_low, low(PIECES))
                sp.dma_start(raw_2[:], w_down).then_inc(s_raw[2], 16)

            load_w(s13, s2)
            for b in range(2, NB):
                load_x(Tile(b))
            def load_expert(e):
                load_w(w13[bass.ds(e.v, 1)].rearrange("o p w n -> p (o w) n"),
                       w2[bass.ds(e.v, 1)].rearrange("o p c n -> p (o c) n"),
                       e.v * 3 + 3, lambda n: e.v * PIECES + n)

            load_expert(Tile(0))
            sp.wait_ge(s_zf, 1)
            zeros = ys[:].rearrange("p e c d -> p (e c d)")
            per = NE * CAP * RW // 128
            share = slots_in[0:NE * CAP, :].rearrange("(p n) d -> p (n d)", p=128)
            step = 2 * CT * D
            for c in range(0, per, step):
                n = min(step, per - c)
                sp.dma_start(share[:, c:c + n], zeros[:, 0:n]).then_inc(s_zero, 16)
            load_expert(Tile(1))
            for grp in range(SH):
                sp.wait_ge(s_ye, GT * (grp + 1) + FREE)
                sp.dma_start(acc[1 + grp * GN:1 + (grp + 1) * GN, :].rearrange("(t p) d -> p t d", p=128),
                             H[:, grp * GT:(grp + 1) * GT, :]).then_inc(s_base, 16)

            def load_xg(e):
                sp.dma_start(xg[:, e.parity], slots_in[bass.ds(e.v * CAP, CAP), :].rearrange(
                    "(t p) d -> p t d", p=128)).then_inc(s_xg[e.parity], 16)

            sp.wait_ge(s_scat, 16 * 2 * NB)
            load_xg(Tile(0))
            load_xg(Tile(1))

            def expert(e):
                sp.wait_ge(s_xt, e.v * CT + CT)
                sp.wait_ge(s_info, e.v * 3 + 3)
                load_xg(e + 2)
                load_expert(e + 2)

            with sp.Fori(0, NE // 2 - 1) as r:
                expert(Tile(0, r))
                expert(Tile(1, r))
            for p in range(2):
                sp.wait_ge(s_add[p], ADDED * (NE // 2) + 16)
            sp.dma_start(out.rearrange("b n d -> (b n) d"), acc[1:1 + N, :]).then_inc(s_out, 16)
            sp.wait_ge(s_out, 16)

        @block.gpsimd
        def _(pool):
            g = nc.gpsimd
            g.memset(ident[:], 0.0).then_inc(s_pc, 1)
            g.memset(causal[:], 0.0).then_inc(s_pc, 1)
            g.memset(headmask[:], 1.0).then_inc(s_pc, 1)
            g.memset(tri[:], 1.0).then_inc(s_pc, 1)
            g.memset(ones[:], 1.0)
            g.memset(eps1[:], 1e-6)
            g.memset(eps2[:], 1e-5)
            g.memset(mhalf[:], -0.5)
            g.memset(segm[:], 1.0).then_inc(s_pc, 1)
            pool.sem_inc(s_lo, FREE)
            pool.wait_ge(s_pc, 5)
            g.affine_select(out=ident[:], in_=ident[:], compare_op=ALU.not_equal, fill=1.0, base=0,
                            pattern=[[-1, 128]], channel_multiplier=1).then_inc(s_pc, 1)
            g.affine_select(out=causal[:], in_=causal[:], compare_op=ALU.is_ge, fill=NEG, base=0,
                            pattern=[[0, HG], [-1, L]], channel_multiplier=1)
            g.affine_select(out=headmask[:], in_=headmask[:], compare_op=ALU.is_ge, fill=0.0, base=0,
                            pattern=[[-HS, 6]], channel_multiplier=1).then_inc(s_pc, 1)
            g.affine_select(out=tri[:], in_=tri[:], compare_op=ALU.is_gt, fill=0.0, base=0,
                            pattern=[[1, 128]], channel_multiplier=-1)
            g.affine_select(out=segm[:], in_=segm[:], compare_op=ALU.is_gt, fill=0.0, base=0,
                            pattern=[[0, NE], [1, NB]], channel_multiplier=0)
            pool.wait_ge(s_pc, 7)
            g.affine_select(out=headmask[:], in_=headmask[:], compare_op=ALU.is_ge, fill=0.0, base=HS - 1,
                            pattern=[[HS, 6]], channel_multiplier=-1)
            g.tensor_copy(identb[:], ident[:])
            g.iota(edesc[:], pattern=[[0, NB], [-1, NE]], base=NE, channel_multiplier=0,
                   allow_small_or_imprecise_dtypes=True)
            g.iota(ebase[:], pattern=[[0, NB], [CAP, NE]], base=0, channel_multiplier=0,
                   allow_small_or_imprecise_dtypes=True)
            g.iota(xn2[:, :, RW - 1], pattern=[[L, NB]], base=1, channel_multiplier=1,
                   allow_small_or_imprecise_dtypes=True)
            g.iota(spare[:], pattern=[[CAP, 2], [128, CT]], base=1 + N, channel_multiplier=1,
                   allow_small_or_imprecise_dtypes=True)
            g.iota(dump[:], pattern=[[N, 2], [L, NB]], base=NE * CAP, channel_multiplier=1,
                   allow_small_or_imprecise_dtypes=True).then_inc(s_cst, 1)
            pool.wait_ge(s_bc, 16 * 3)

            def rsqrt(n, eps, done, b, stats):
                pool.wait_ge(s_l3 if n == 2 else s_ln, stats)
                g.tensor_tensor(ve[:, n], mv[:, n, 1:2], eps[:], ALU.add).then_inc(done, 1)
                pool.wait_ge(done, b.v * 2 + 1)
                g.tensor_tensor(rstd[:, n], ve[:, n], mhalf[:], ALU.pow).then_inc(done, 1)

            def split_lo(job, par, n):
                m, k = (n // 4, n % 4) if n < 8 else (2, n - 8)
                half, cols = k // 2, slice(k % 2 * (INNER // 2), (k % 2 + 1) * (INNER // 2))
                if m == 0:
                    lo, raw, hi = wa[:, par, 1, half, cols], raw_a[:, half, cols], wa[:, par, 0, half, cols]
                elif m == 1:
                    lo, raw, hi = wb_lo[:, par, half, cols], raw_b[0:DB, half, cols], wb_hi[0:DB, par, half, cols]
                else:
                    pair = slice(2 * k, 2 * k + 2)
                    lo, raw, hi = w2s[:, par, pair, 1], raw_2[:, pair], w2s[:, par, pair, 0]
                pool.wait_ge(s_hiw, job * 3 + (m + 1))
                g.tensor_tensor(lo, raw, hi.bitcast(F32), ALU.subtract).then_inc(s_low, 1)

            def g_lo(u, par, c, c0, n):
                pool.wait_ge(s_hi, u + 1)
                g.tensor_tensor(G[:, 1, c, c0:c0 + n], gf[:, par, 0:n], G[:, 0, c, c0:c0 + n].bitcast(F32),
                                ALU.subtract).then_inc(s_lo, 1)

            def norm(b, k):
                pool.wait_ge(s_rinv, b.v * NG + (k + 1))
                g.tensor_tensor(probs[:, k], probs[:, k],
                                rinv[:, HG * k:HG * (k + 1)].unsqueeze(2).to_broadcast([128, HG, L]),
                                ALU.mult).then_inc(s_norm, 1)

            def step(i):
                b = i
                if b.inside():
                    norm(b, 0)
                n = i + 2
                if n.inside():
                    rsqrt(0, eps1, s_r1, n, n.v * 7 + 2)
                if b.inside():
                    norm(b, 1)
                    norm(b, 2)
                    norm(b, 3)
                if n.inside():
                    rsqrt(1, eps2, s_r2, n, n.v * 7 + 6)
                    pool.wait_ge(s_relu, n.v + 1)
                    g.tensor_tensor(H[:, bass.ds(n.v, 1)].rearrange("p o d -> p (o d)"), h1[:], bproj_bc[:],
                                    ALU.add).then_inc(s_h1b, 1)
                m = i + -1
                if m.inside():
                    rsqrt(2, eps2, s_r3, m, m.v * 5 + 3)
                if i.reg is None and i.const == 0:
                    for n in range(PIECES):
                        split_lo(0, 0, n)

            steps(pool, step)

            pool.wait_ge(s_zf, 1)
            for p in range(2):
                pool.dma_start(acc[1 + N + p * CAP:1 + N + (p + 1) * CAP, :].rearrange("(t p) d -> p t d", p=128),
                               ys[:, p]).then_inc(s_add[p], 16)
            done = 0

            def all_sums():
                nonlocal done
                done += 1
                pool.wait_ge(s_cnt, done)
                g.partition_all_reduce(tot[:].rearrange("p k e -> p (k e)"), cnt[:].rearrange("p k e -> p (k e)"),
                                       128, RADD).then_inc(s_tot, 1)

            for grp in range(POOL_LO):
                for c in range(IC):
                    if search_at(grp, chunk=c):
                        all_sums()
                    g_lo(grp * IC + c, c % 2, c, 0, GN)
                    if grp * IC + c < PIECES:
                        split_lo(1, 1, grp * IC + c)
                for t in range(GT):
                    if search_at(grp, tile=t):
                        all_sums()
            all_sums()

            pool.wait_ge(s_zero, 16 * N_ZERO)
            pool.wait_ge(s_hc, NB)
            pool.wait_ge(s_wt, 1)
            for j in range(2):
                pool.wait_ge(s_ix, j + 1)
                for t in range(NB):
                    pool.indirect_dma_start(slots_in, bass.IndirectOffsetOnAxis(ap=dst_i[:, j, t:t + 1], axis=0),
                                            xn2[:, t, :], None).then_inc(s_scat, 16)

            def rows_ready(e, t):
                if t == 0:
                    before = e.pair if e.parity == 0 else e.pair + 1
                    pool.wait_ge(s_add[1 - e.parity], before * ADDED + 16)
                pool.wait_ge(s_ye, e.v * CT + (D_E0 + t + 1 + FREE))

            def add_rows(e, t):
                pool.indirect_dma_start(acc, bass.IndirectOffsetOnAxis(ap=row_i[:, e.parity, t:t + 1], axis=0),
                                        ys[:, e.parity, t, :], None, compute_op=ALU.add,
                                        ).then_inc(s_add[e.parity], 16)

            def expert(e, more):
                for c in range(IC):
                    g_lo(e.v * (2 * IC) + (U_E0 + IC + c), c % 2, c, HALF, HALF)
                    if 1 <= c <= EARLY and more:
                        split_lo(e.v + 2, e.parity, c - 1)
                if more:
                    for n in range(EARLY, PIECES - CT):
                        split_lo(e.v + 2, e.parity, n)
                for t in range(CT):
                    rows_ready(e, t)
                    if more:
                        split_lo(e.v + 2, e.parity, PIECES - CT + t)
                    add_rows(e, t)

            pool.wait_ge(s_base, 16 * SH)
            with pool.Fori(0, NE // 2 - 1) as r:
                expert(Tile(0, r), True)
                expert(Tile(1, r), True)
            expert(Tile(NE - 2), True)
            expert(Tile(NE - 1), False)

        @block.scalar
        def _(act):
            s = nc.scalar

            def exp(b, k):
                act.wait_ge(s_max, b.v * NG + (k + 1))
                if b.after(1):
                    act.wait_ge(s_ptm, b.v * NG + (k + 1 - NG))
                for h in range(HG):
                    c = HG * k + h
                    last = s.activation(probs[:, k, h], bank_s[k][:, h * L:(h + 1) * L], ACT.Exp,
                                        bias=nmax[:, c:c + 1], accum_out=rsum[:, c:c + 1])
                last.then_inc(s_exp, 1)

            def evac_qv(b):
                act.wait_ge(s_qvm, b.v + 1)
                if b.after(1):
                    act.wait_ge(s_s, b.v * NG)
                s.activation(qT[:].rearrange("p c n -> p (c n)"), bank_qv[0:DC, 0:2 * L], ACT.Copy,
                             scale=float(HS) ** -0.5).then_inc(s_qv, 1)
                if b.after(2):
                    act.wait_ge(s_pv, b.v - 1)
                s.activation(vs[:, b.parity, :, 0:HS], bank_qv[:, 2 * L:2 * L + D].rearrange(
                    "p (h d) -> p h d", h=NH), ACT.Copy).then_inc(s_qv, 1)

            def relu(b):
                act.wait_ge(s_ln, b.v * 7 + 4)
                if b.after(1):
                    act.wait_ge(s_h1b, b.v)
                s.activation(h1[:], un[:], ACT.Relu).then_inc(s_relu, 1)

            def evac_pt(b, k):
                act.wait_ge(s_ptm, b.v * NG + (k + 1))
                if b.after(1):
                    act.wait_ge(s_pv, b.v)
                s.activation(pT[:, HG * k:HG * (k + 1)].rearrange("p h n -> p (h n)"),
                             bank_s[k][:, 0:HG * L], ACT.Copy).then_inc(s_pt, 1)

            def evac_o(b):
                act.wait_ge(s_pv, b.v + 1)
                if b.after(1):
                    act.wait_ge(s_proj, b.v)
                s.activation(oT[:].rearrange("p h n -> p (h n)"), bank_o[:, 0:HG * L], ACT.Copy).then_inc(s_o, 1)

            def evac_t2(b):
                act.wait_ge(s_t2, b.v + 1)
                s.activation(xs[:, HI_A:HI_LO_B + 1, bass.ds(b.v * L, L)],
                             bank_k[:, 0:2 * L].rearrange("p (c n) -> p c n", c=2), ACT.Copy).then_inc(s_xn2t, 1)

            def copy_rows(b):
                act.wait_ge(s_l3, b.v * 5 + 5)
                s.activation(H[:, bass.ds(b.v, 1)].rearrange("p o d -> p (o d)"), hrow[:], ACT.Copy)
                s.activation(xn2[:, bass.ds(b.v, 1), 0:DW].rearrange("p o d -> p (o d)"), xn2s[:], ACT.Copy).then_inc(s_hc, 1)

            def evac_t1(b):
                act.wait_ge(s_t1, b.v + 1)
                if b.after(1):
                    act.wait_ge(s_qvm, b.v)
                s.activation(xnT[0:DC].rearrange("p c n -> p (c n)"), bank_qv[0:DC, 0:2 * L],
                             ACT.Copy).then_inc(s_xnt, 1)

            def step(i):
                if i.inside():
                    exp(i, 0)
                if (i + -2).inside():
                    evac_t2(i + -2)
                if (i + 1).inside():
                    evac_t1(i + 1)
                if i.inside():
                    for k in range(1, NG):
                        exp(i, k)
                if (i + 1).inside():
                    evac_qv(i + 1)
                if (i + 2).inside():
                    relu(i + 2)
                if i.inside():
                    for k in range(NG):
                        evac_pt(i, k)
                    evac_o(i)
                if (i + -1).inside():
                    copy_rows(i + -1)
                if i.reg is None and i.const == 0:
                    split_hi(0)

            def split_hi(job, par=0, n=None):
                for k, (hi, raw) in enumerate(((wa[:, par, 0], raw_a[:]), (wb_hi[:, par], raw_b[:]),
                                               (w2s[:, par, :, 0], raw_2[:]))):
                    if n is None or k == n:
                        loads = 32 if k == 1 else 16
                        act.wait_ge(s_raw[k], job * loads + loads)
                        s.activation(hi, raw, ACT.Copy).then_inc(s_hiw, 1)

            act.wait_ge(s_cd, 4)
            steps(act, step)

            for k in range(N // 512):
                act.wait_ge(s_lg, k + 1)
                s.activation(lgT[:, 512 * k:512 * (k + 1)], up_a[k % 2][0:NE, 0:512], ACT.Copy).then_inc(s_lgc, 1)
            act.wait_ge(s_rt, 2)
            s.activation(RT[1][:], RT[1][:], ACT.Exp).then_inc(s_rex, 1)

            def silu(u, u_par, n):
                act.wait_ge(s_u, u + 1)
                act.wait_ge(s_mul, u + 1)
                s.activation(sg[:, u_par, 0:n], up_a[u_par][:, 0:n], ACT.Silu).then_inc(s_silu, 1)

            for c in range(IC):
                silu(c, c % 2, GN)
                if 1 <= c < 4:
                    split_hi(1, 1, c - 1)
            with act.Fori(1, SH) as grp:
                for c in range(IC):
                    silu(grp * IC + c, c % 2, GN)

            def expert(e, more):
                for hf in range(2):
                    for c in range(IC):
                        silu(e.v * (2 * IC) + (U_E0 + hf * IC + c), c % 2, HALF)
                        if hf == 0 and c == 3 and more:
                            act.wait_ge(s_d, e.v * CT + D_E0)
                        if HI_AT <= hf * IC + c < HI_AT + 3 and more:
                            split_hi(e.v + 2, e.parity, hf * IC + c - HI_AT)
                for t in range(CT):
                    if t == 0:
                        act.wait_ge(s_add[e.parity], e.pair * ADDED + 16)
                        act.wait_ge(s_info, e.v * 3 + 3)
                    act.wait_ge(s_d, e.v * CT + (D_E0 + t + 1))
                    s.activation(ys[:, e.parity, t, :], down[(e.const * CT + t) % 2][:, 0:D],
                                 ACT.Copy, scale=wslot[:, e.parity, t:t + 1]).then_inc(s_y1, 1)

            act.wait_ge(s_zero, 16 * N_ZERO)
            for p in range(2):
                act.wait_ge(s_add[p], 16)
            with act.Fori(0, NE // 2 - 1) as r:
                expert(Tile(0, r), True)
                expert(Tile(1, r), True)
            expert(Tile(NE - 2), True)
            expert(Tile(NE - 1), False)

        @block.tensor
        def _(pe):
            mm = nc.tensor.matmul

            def rows(c):
                return slice(0, DC + c)

            def pointwise(b):
                pe.wait_ge(s_conv, b.v * 14 + 14)
                if b.after(1):
                    pe.wait_ge(s_ln, b.v * 7 - 4)
                for c in range(2):
                    last = mm(bank_y[:, 0:D], cv[rows(c), b.parity, c], pw_sb[rows(c), c], start=c == 0, stop=c == 1)
                last.then_inc(s_y, 1)

            def turn_xn(b):
                pe.wait_ge(s_ln, b.v * 7 + 7)
                if b.after(1):
                    pe.wait_ge(s_qv, b.v * 2)
                for c in range(2):
                    last = nc.tensor.transpose(bank_qv[0:DC, c * L:(c + 1) * L], xn[:, c * DC:(c + 1) * DC], ident[:])
                last.then_inc(s_t1, 1)

            def qkv(b):
                pe.wait_ge(s_xnt, b.v + 1)
                if b.after(3):
                    pe.wait_ge(s_xlo, b.v * 2 - 4)
                if b.after(1):
                    pe.wait_ge(s_kbd, b.v * 2)
                for m in range(2):
                    for c in range(2):
                        last = mm(bank_k[0:DC, m * L:(m + 1) * L], wqkv_sb[rows(c), c, D + m * DC:D + (m + 1) * DC],
                                  xnT[rows(c), c], start=c == 0, stop=c == 1)
                last.then_inc(s_k, 1)
                for m in range(2):
                    for c in range(2):
                        mm(bank_qv[0:DC, m * L:(m + 1) * L], wqkv_sb[rows(c), c, m * DC:(m + 1) * DC],
                           xnT[rows(c), c], start=c == 0, stop=c == 1)
                for c in range(2):
                    last = mm(bank_qv[:, 2 * L:2 * L + D], xnT[rows(c), c], wqkv_sb[rows(c), c, 2 * D:3 * D],
                              start=c == 0, stop=c == 1)
                last.then_inc(s_qvm, 1)

            def scores(b, banks):
                if banks[0] == 0:
                    pe.wait_ge(s_qv, b.v * 2 + 1)
                    pe.wait_ge(s_kbd, b.v * 2 + 2)
                for k in banks:
                    if b.after(1):
                        pe.wait_ge(s_pt, b.v * NG + (k + 1 - NG))
                    m, h0 = k // 2, HG * (k % 2)
                    mm(bank_s[k][:, 0:HG * L], qT[:, m], kbd[:, m, h0:h0 + HG].rearrange("p h n -> p (h n)"),
                       start=True, stop=False)
                    mm(bank_s[k][:, 0:HG * L], identb[:], causal[:].rearrange("p h n -> p (h n)"),
                       start=False, stop=True).then_inc(s_s, 1)

            def turn_p(b):
                for k in range(NG):
                    pe.wait_ge(s_norm, b.v * NG + (k + 1))
                    for h in range(HG):
                        last = nc.tensor.transpose(bank_s[k][:, h * L:(h + 1) * L], probs[:, k, h], ident[:])
                    last.then_inc(s_ptm, 1)

            def pv(b):
                pe.wait_ge(s_qv, b.v * 2 + 2)
                pe.wait_ge(s_pt, b.v * NG + NG)
                if b.after(1):
                    pe.wait_ge(s_l3, b.v * 5 - 4)
                for h in range(NH):
                    j, q = h // 4, h % 4
                    last = mm(bank_o[32 * q:32 * q + 32, j * L:(j + 1) * L], vs[:, b.parity, h], pT[:, h],
                              start=True, stop=True)
                last.then_inc(s_pv, 1)

            def project(b):
                pe.wait_ge(s_o, b.v + 1)
                for j in range(HG):
                    last = mm(bank_o[:, 0:D], oT[:, j], wproj_sb[:, j], start=j == 0, stop=j == HG - 1)
                last.then_inc(s_proj, 1)

            def turn_xn2(b):
                pe.wait_ge(s_l3, b.v * 5 + 5)
                if b.reg is not None or b.const + 2 < NB:
                    pe.wait_ge(s_kbd, b.v * 2 + 6)
                if b.after(1):
                    pe.wait_ge(s_xlo, b.v * 2)
                for c in range(2):
                    last = nc.tensor.transpose(bank_k[:, c * L:(c + 1) * L], xn2s[:, c * DA:(c + 1) * DA], ident[:])
                last.then_inc(s_t2, 1)

            def step(i):
                if i.inside():
                    scores(i, (0, 1))
                if (i + -2).inside():
                    turn_xn2(i + -2)
                if (i + 1).inside():
                    turn_xn(i + 1)
                if i.inside():
                    scores(i, (2, 3))
                if (i + -1).inside():
                    project(i + -1)
                if (i + 1).inside():
                    qkv(i + 1)
                if i.inside():
                    turn_p(i)
                if (i + 3).inside():
                    pointwise(i + 3)
                if i.inside():
                    pv(i)

            pe.wait_ge(s_cst, 1)
            pe.wait_ge(s_cd, 4)
            pe.wait_ge(s_wa, 16 * N_WA)
            steps(pe, step)

            def split_product(bank, w, x):
                hi_a, lo_a, hi_b, lo_b = w
                mm(bank, hi_a, x(HI_A), start=True, stop=False)
                mm(bank, hi_a, x(LO_A), start=False, stop=False)
                mm(bank, lo_a, x(HI_A), start=False, stop=False)
                mm(bank, hi_b, x(HI_LO_B), start=False, stop=False)
                return mm(bank, lo_b, x(HI_LO_B, DB), start=False, stop=True)

            def tokens(c0):
                return lambda part, rows=128: xs[0:rows, part, bass.ds(c0, GN)]

            pe.wait_ge(s_wrs, 5)
            pe.wait_ge(s_xlo, 2 * NB)
            for k in range(N // GN):
                if k >= 2:
                    pe.wait_ge(s_lgc, k - 1)
                split_product(up_a[k % 2][:, 0:GN], (wr_sp[:, 0], wr_sp[:, 2], wr_sp[:, 1], wr_sp[0:DB, 3]),
                              tokens(GN * k)).then_inc(s_lg, 1)
            pe.wait_ge(s_lgc, N // 512)
            for t in range(NB):
                last = nc.tensor.transpose(turn[0][:, t * NE:(t + 1) * NE], lgT[:, t * L:(t + 1) * L], ident[0:NE, 0:NE])
            last.then_inc(s_lgt, 1)

            def up(u, par, w, c, x, n):
                cs = slice(c * 128, (c + 1) * 128)
                pe.wait_ge(s_mul, u + 1)
                for k, bank in enumerate((up_a, up_b)):
                    last = split_product(bank[par][:, 0:n], (wa[:, w, 0, k, cs], wa[:, w, 1, k, cs],
                                                             wb_hi[:, w, k, cs], wb_lo[:, w, k, cs]), x)
                last.then_inc(s_u, 1)

            def down_tile(d, par, u_done, c0, w):
                pe.wait_ge(s_lo, u_done + FREE)
                pe.wait_ge(s_ye, d + 1)
                for c in range(IC):
                    hi, lo = G[:, 0, c, c0:c0 + 128], G[:, 1, c, c0:c0 + 128]
                    mm(down[par][:, 0:2 * D], hi, w2s[:, w, c].rearrange("p h d -> p (h d)"), start=c == 0,
                       stop=False)
                    last = mm(down[par][:, 0:D], lo, w2s[:, w, c, 0], start=False, stop=c == IC - 1)
                last.then_inc(s_d, 1)

            def ranks(n):
                pe.wait_ge(s_pre, 2 * n + 1)
                m = RT[4 + n]
                mm(turn[1][:, 0:NB * NE], tri[:], m[:].rearrange("p t e -> p (t e)"), start=True, stop=True)
                mm(turn[1][:, 128:128 + NB * NE], ones[:], m[:].rearrange("p t e -> p (t e)"),
                   start=True, stop=True).then_inc(s_lgt, 1)

            def shared(grp, counts=False):
                for c in range(IC):
                    up(grp * IC + c, c % 2, 0, c, tokens(grp * GN), GN)
                    if counts and c % 2 == 0 and c < 4:
                        ranks(c // 2)
                for t in range(GT):
                    down_tile(grp * GT + t, t % 2, grp * IC + IC, t * 128, 0)

            pe.wait_ge(s_low, PIECES)
            with pe.Fori(0, POOL_LO) as grp:
                shared(grp)
            for grp in range(POOL_LO, SH):
                shared(grp, grp == POOL_LO)

            def turn_slots(e, t):
                if t == 0:
                    pe.wait_ge(s_xg[e.parity], e.pair * 16 + 16)
                if e.reg is not None or e.const * CT + t >= 2:
                    pe.wait_ge(s_xte, e.v * CT + (t - 1))
                for c in range(2):
                    last = nc.tensor.transpose(turn[(e.const * CT + t) % 2][:, c * 128:(c + 1) * 128],
                                               xg[:, e.parity, t, c * DA:(c + 1) * DA], ident[:])
                last.then_inc(s_xt, 1)

            def expert(e, more):
                p, w = e.parity, (e + 1).parity
                pe.wait_ge(s_low, e.v * PIECES + (PIECES + 8))
                pe.wait_ge(s_xte, e.v * CT + CT)
                for hf in range(2):
                    for c in range(IC):
                        up(e.v * (2 * IC) + (U_E0 + hf * IC + c), c % 2, w, c,
                           lambda part, rows=128: xgs[0:rows, p, part, hf * HALF:(hf + 1) * HALF], HALF)
                        if hf == 1 and c < CT and more:
                            turn_slots(e + 1, c)
                pe.wait_ge(s_low, e.v * PIECES + 2 * PIECES)
                for t in range(CT):
                    u_done = U_E0 + (IC if (t + 1) * 128 <= HALF else 2 * IC)
                    down_tile(e.v * CT + (D_E0 + t), (e.const * CT + t) % 2, e.v * (2 * IC) + u_done, t * 128, w)

            for t in range(CT):
                turn_slots(Tile(0), t)
            with pe.Fori(0, NE // 2 - 1) as r:
                expert(Tile(0, r), True)
                expert(Tile(1, r), True)
            expert(Tile(NE - 2), True)
            expert(Tile(NE - 1), False)

        @block.vector
        def _(dve):
            v = nc.vector
            v.memset(cv[DC:DC + 1, :, 1, :], 1.0).then_inc(s_cd, 1)
            v.memset(xnT[DC:DC + 1, 1, :], 1.0).then_inc(s_cd, 1)
            v.memset(vs[:], 0.0).then_inc(s_cd, 1)
            v.memset(wr_sp[:].bitcast(F32), 0.0).then_inc(s_wrs, 1)
            v.memset(thr[:], 0).then_inc(s_cd, 1)
            for k in range(3):
                v.memset(digit[:, k], (k + 1) << (BITS - 2)).then_inc(s_cd, 1)
            dve.wait_ge(s_cst, 1)
            dve.wait_ge(s_wa, 16 * N_WA)
            dve.wait_ge(s_bc, 16 * 3)
            dve.sem_inc(s_mul, FREE)
            dve.sem_inc(s_ye, FREE)

            def conv(b, part):
                taps = [range(0, 2), range(2, 4), range(4, 6), range(6, 7)][part]
                if part == 0:
                    dve.wait_ge(s_x[b.parity], b.pair * 16 + 16)
                    if b.after(2):
                        dve.wait_ge(s_y, b.v - 1)
                for k in taps:
                    for c in range(2):
                        acc, src = cv[0:DC, b.parity, c], xb[:, b.parity, c, k:k + L]
                        if k == 0:
                            v.tensor_scalar(acc, src, dw_sb[:, c, k:k + 1], None, ALU.mult).then_inc(s_conv, 1)
                        else:
                            dve.wait_ge(s_conv, b.v * 14 + (2 * k + c - 1))
                            v.scalar_tensor_tensor(acc, src, dw_sb[:, c, k:k + 1], acc, ALU.mult,
                                                   ALU.add).then_inc(s_conv, 1)

            def maxima(b, k):
                dve.wait_ge(s_s, b.v * NG + (k + 1))
                v.tensor_reduce(nmax[:, HG * k:HG * (k + 1)], bank_s[k][:, 0:HG * L].rearrange(
                    "p (h n) -> p h n", h=HG), AX.X, ALU.max, negate=True).then_inc(s_max, 1)

            def inverse(b, k):
                dve.wait_ge(s_exp, b.v * NG + (k + 1))
                if b.after(1):
                    dve.wait_ge(s_norm, b.v * NG + (k + 1 - NG))
                v.reciprocal(rinv[:, HG * k:HG * (k + 1)], rsum[:, HG * k:HG * (k + 1)]).then_inc(s_rinv, 1)

            def keys(b, m):
                if m == 0:
                    dve.wait_ge(s_k, b.v + 1)
                    if b.after(1):
                        dve.wait_ge(s_s, b.v * NG)
                v.tensor_tensor(kbd[:, m], bank_k[0:DC, m * L:(m + 1) * L].unsqueeze(1).to_broadcast([DC, 6, L]),
                                headmask[:].unsqueeze(2).to_broadcast([DC, 6, L]), ALU.mult).then_inc(s_kbd, 1)

            def ln1_stats(b):
                dve.wait_ge(s_y, b.v + 1)
                v.bn_stats(st[:, 0], bank_y[:, 0:D]).then_inc(s_ln, 1)
                dve.wait_ge(s_ln, b.v * 7 + 1)
                if b.after(1):
                    dve.wait_ge(s_r1, b.v * 2)
                v.memset(carry[:, 0:1], 0.0)
                v.bn_aggr(mv[:, 0], st[:, 0]).then_inc(s_ln, 1)
                dve.wait_ge(s_ln, b.v * 7 + 2)

            def ln1_apply(b):
                v.scalar_tensor_tensor(tn[:], bank_y[:, 0:D], mv[:, 0, 0:1], g_bc[:], ALU.subtract,
                                       ALU.mult).then_inc(s_ln, 1)
                dve.wait_ge(s_ln, b.v * 7 + 3)
                dve.wait_ge(s_r1, b.v * 2 + 2)
                if b.after(1):
                    dve.wait_ge(s_relu, b.v)
                v.scalar_tensor_tensor(un[:], tn[:], rstd[:, 0], b_bc[:], ALU.mult, ALU.add).then_inc(s_ln, 1)

            def ln2_stats(b):
                dve.wait_ge(s_relu, b.v + 1)
                v.bn_stats(st[:, 1], h1[:]).then_inc(s_ln, 1)
                dve.wait_ge(s_ln, b.v * 7 + 5)
                if b.after(1):
                    dve.wait_ge(s_r2, b.v * 2)
                v.memset(carry[:, 1:2], 0.0)
                v.bn_aggr(mv[:, 1], st[:, 1]).then_inc(s_ln, 1)
                dve.wait_ge(s_ln, b.v * 7 + 6)

            def ln2_apply(b):
                dve.wait_ge(s_r2, b.v * 2 + 2)
                if b.after(1):
                    dve.wait_ge(s_t1, b.v)
                v.tensor_scalar(xn[:], h1[:], mv[:, 1, 0:1], rstd[:, 1], ALU.subtract, ALU.mult).then_inc(s_ln, 1)

            def split_wr():
                dve.wait_ge(s_sw, 48)
                dve.wait_ge(s_wrs, 1)
                v.tensor_copy(wr_sp[:, 0:2, 0:NE], wr_raw[:]).then_inc(s_wrs, 2)
                dve.wait_ge(s_wrs, 3)
                v.tensor_tensor(wr_sp[:, 2:4, 0:NE], wr_raw[:], wr_sp[:, 0:2, 0:NE].bitcast(F32),
                                ALU.subtract).then_inc(s_wrs, 2)

            def lo_rows(b):
                cols = bass.ds(b.v * L, L)
                dve.wait_ge(s_xn2t, b.v + 1)
                v.tensor_tensor(xs[:, LO_A, cols], bank_k[:, 0:L], xs[:, HI_A, cols].bitcast(F32),
                                ALU.subtract).then_inc(s_xlo, 1)
                v.tensor_tensor(xs[DB:128, HI_LO_B, cols], bank_k[DB:128, L:2 * L],
                                xs[DB:128, HI_LO_B, cols].bitcast(F32), ALU.subtract).then_inc(s_xlo, 1)

            def ln3(b):
                row = H[:, bass.ds(b.v, 1)].rearrange("p o d -> p (o d)")
                dve.wait_ge(s_proj, b.v + 1)
                dve.wait_ge(s_h1b, b.v + 1)
                if b.after(1):
                    dve.wait_ge(s_hc, b.v)
                v.tensor_tensor(hrow[:], bank_o[:, 0:D], row, ALU.add).then_inc(s_l3, 1)
                dve.wait_ge(s_l3, b.v * 5 + 1)
                v.bn_stats(st[:, 2], hrow[:]).then_inc(s_l3, 1)
                dve.wait_ge(s_l3, b.v * 5 + 2)
                v.memset(carry[:, 2:3], 0.0)
                v.bn_aggr(mv[:, 2], st[:, 2]).then_inc(s_l3, 1)

            def ln3_apply(b):
                dve.wait_ge(s_l3, b.v * 5 + 3)
                dve.wait_ge(s_r3, b.v * 2 + 2)
                if b.after(1):
                    dve.wait_ge(s_t2, b.v)
                for cols, src in ((slice(0, D), slice(0, D)), (slice(D, DW), slice(DA, D))):
                    v.tensor_scalar(xn2s[:, cols], hrow[:, src], mv[:, 2, 0:1], rstd[:, 2], ALU.subtract,
                                    ALU.mult).then_inc(s_l3, 1)

            def taps(x, parts):
                if x.inside():
                    for part in parts:
                        conv(x, part)

            def step(i):
                a, n, x, m = i, i + 2, i + 4, i + -1
                taps(x, [0])
                if a.inside():
                    maxima(a, 0)
                taps(x, [1])
                if a.inside():
                    maxima(a, 1)
                if (i + -2).inside():
                    lo_rows(i + -2)
                if a.inside():
                    maxima(a, 2)
                    inverse(a, 0)
                    maxima(a, 3)
                    inverse(a, 1)
                if n.inside():
                    ln1_stats(n)
                if (i + 1).inside():
                    keys(i + 1, 0)
                if a.inside():
                    inverse(a, 2)
                if n.inside():
                    ln1_apply(n)
                if a.inside():
                    inverse(a, 3)
                if (i + 1).inside():
                    keys(i + 1, 1)
                if m.inside():
                    ln3(m)
                if n.inside():
                    ln2_stats(n)
                taps(x, [2, 3])
                if m.inside():
                    ln3_apply(m)
                if n.inside():
                    ln2_apply(n)

            split_wr()
            steps(dve, step)
            dve.wait_ge(s_proj, NB)
            dve.wait_ge(s_hc, NB)
            v.memset(ys[:].rearrange("p e t d -> p (e t d)"), 0.0).then_inc(s_zf, 1)

            chain = [0]

            def link(ins, k=1):
                chain[0] += 1
                ins.then_inc(s_rt, 1)
                dve.wait_ge(s_rt, chain[0])

            def wide(ap):
                return ap.unsqueeze(2).to_broadcast([128, NB, NE])

            def softmax():
                dve.wait_ge(s_lgt, 1)
                lg = turn[0][:, 0:NB * NE].rearrange("p (t e) -> p t e", e=NE)
                link(v.tensor_reduce(RS[0][:], lg, AX.X, ALU.max))
                link(v.tensor_tensor(RT[1][:], lg, wide(RS[0][:]), ALU.subtract))
                dve.wait_ge(s_rex, 1)
                link(v.tensor_reduce(RS[1][:], RT[1][:], AX.X, ALU.add))
                link(v.reciprocal(RS[2][:], RS[1][:]))
                link(v.tensor_tensor(RT[0][:], RT[1][:], wide(RS[2][:]), ALU.mult))

            def best(j):
                link(v.tensor_reduce(RS[j][:], RT[0][:], AX.X, ALU.max))
                link(v.tensor_tensor(RT[1][:], RT[0][:], wide(RS[j][:]), ALU.is_equal))
                link(v.tensor_tensor(RT[1][:], RT[1][:], edesc[:], ALU.mult))
                link(v.tensor_reduce(RS[2][:], RT[1][:], AX.X, ALU.max))
                link(v.tensor_tensor(oh[:, j], edesc[:], wide(RS[2][:]), ALU.is_equal))

            def first_choice():
                best(0)
                link(v.scalar_tensor_tensor(RT[0][:].rearrange("p t e -> p (t e)"),
                                            oh[:, 0].rearrange("p t e -> p (t e)"), -2.0,
                                            RT[0][:].rearrange("p t e -> p (t e)"), ALU.mult, ALU.add))
            def second_choice():
                best(1)
                link(v.tensor_tensor(RS[2][:], RS[0][:], RS[1][:], ALU.add))
                link(v.tensor_scalar(RS[2][:], RS[2][:], 1e-9, None, ALU.max))
                link(v.reciprocal(RS[3][:], RS[2][:]))
                for j in range(2):
                    link(v.tensor_tensor(wgt[:, j], RS[j][:], RS[3][:], ALU.mult))
                    link(v.tensor_tensor(RT[1 + j][:], oh[:, j], wide(wgt[:, j]), ALU.mult))
                link(v.tensor_tensor(RT[3][:], oh[:, 0], oh[:, 1], ALU.add))
                link(v.tensor_tensor(RT[1][:], RT[1][:], RT[2][:], ALU.add))
                link(v.scalar_tensor_tensor(score[:].rearrange("p t e -> p (t e)"),
                                            RT[3][:].rearrange("p t e -> p (t e)"), 1.0,
                                            RT[1][:].rearrange("p t e -> p (t e)"), ALU.subtract, ALU.add))
                v.tensor_copy(xn2[:, :, DW:DW + NE], RT[1][:]).then_inc(s_wt, 1)

            def over(ap):
                return ap.unsqueeze(1).to_broadcast([128, NB, NE])

            def search_count():
                k = len(searched)
                searched.append(k)
                w = 8 * k
                v.tensor_tensor(cand[:], thr[:].unsqueeze(1).to_broadcast([128, 3, NE]), digit[:],
                                ALU.bitwise_or).then_inc(s_thr, 1)
                dve.wait_ge(s_thr, w + 1)
                v.tensor_tensor(above[:], score[:].unsqueeze(1).to_broadcast([128, 3, NB, NE]),
                                cand[:].bitcast(F32).unsqueeze(2).to_broadcast([128, 3, NB, NE]),
                                ALU.is_ge).then_inc(s_thr, 1)
                v.tensor_scalar(digit[:], digit[:], 2, None, ALU.logical_shift_right).then_inc(s_thr, 1)
                dve.wait_ge(s_thr, w + 3)
                v.tensor_reduce(cnt[:], above[:].rearrange("p k t e -> p k e t"), AX.X, ALU.add).then_inc(s_cnt, 1)

            def search_take():
                k = len(searched) - 1
                w = 8 * k
                dve.wait_ge(s_tot, k + 1)
                v.tensor_scalar(ge[:], tot[:], float(CAP), None, ALU.is_ge).then_inc(s_thr, 1)
                for m in range(3):
                    dve.wait_ge(s_thr, w + 4 + m)
                    v.copy_predicated(thr[:], ge[:, m], cand[:, m]).then_inc(s_thr, 1 if m < 2 else 2)
                dve.wait_ge(s_thr, w + 8)

            searched = []

            def gated(u, par, c, c0, n, lo=False):
                dve.wait_ge(s_silu, u + 1)
                dve.wait_ge(s_lo, u + 1)
                v.tensor_tensor(gf[:, par, 0:n], sg[:, par, 0:n], up_b[par][:, 0:n], ALU.mult).then_inc(s_mul, 1)
                dve.wait_ge(s_mul, u + (FREE + 1))
                v.tensor_copy(G[:, 0, c, c0:c0 + n], gf[:, par, 0:n]).then_inc(s_hi, 1)
                if lo:
                    dve.wait_ge(s_hi, u + 1)
                    dve.wait_ge(s_lo, u + FREE)
                    v.tensor_tensor(G[:, 1, c, c0:c0 + n], gf[:, par, 0:n], G[:, 0, c, c0:c0 + n].bitcast(F32),
                                    ALU.subtract).then_inc(s_lo, 1)

            def add_shared(d, par, tile):
                dve.wait_ge(s_d, d + 1)
                row = H[:, tile]
                v.tensor_tensor(row, down[par][:, 0:D], row, ALU.add).then_inc(s_sh, 1)
                dve.wait_ge(s_sh, d + 1)
                v.tensor_tensor(row, down[par][:, D:2 * D], row, ALU.add).then_inc(s_ye, 1)

            def masks():
                t = thr[:].bitcast(F32)
                link(v.tensor_tensor(RT[3][:], score[:], over(t), ALU.is_gt))
                link(v.tensor_reduce(cnt[:, 0], RT[3][:].rearrange("p t e -> p e t"), AX.X, ALU.add))
                v.sem_inc(s_cnt, 1)
                v.tensor_tensor(RT[4][:], score[:], over(t), ALU.is_equal).then_inc(s_pre, 1)

            def ranks(n, mask, res):
                dve.wait_ge(s_lgt, 2 + n)
                by_e = "p t e -> p e t"
                all_p = turn[1][:, 128:128 + NB * NE].rearrange("p (t e) -> p e t", e=NE)
                tr = RT[6][:].rearrange("p t e -> p (t e)").rearrange("p (e t) -> p e t", e=NE)
                flat = "p e t -> p (e t)"
                link(v.tensor_copy(tr, all_p))
                sc = RT[7][:].rearrange("p t e -> p (t e)")
                link(v.tensor_tensor_scan(sc, segm[:].rearrange(flat), tr.rearrange(flat), 0.0, ALU.mult, ALU.add))
                link(v.tensor_tensor(sc, sc, tr.rearrange(flat), ALU.subtract))
                link(v.tensor_tensor(res, turn[1][:, 0:NB * NE].rearrange("p (t e) -> p t e", e=NE),
                                     sc.rearrange("p (e t) -> p t e", e=NE), ALU.add))

            def keep():
                ranks(0, RT[4], RT[1][:])
                dve.wait_ge(s_tot, BITS // 2 + 1)
                link(v.tensor_tensor(RT[1][:], RT[1][:], over(tot[:, 0]), ALU.add))
                link(v.tensor_scalar(RT[1][:], RT[1][:], float(CAP), None, ALU.is_lt))
                link(v.tensor_tensor(RT[1][:], RT[1][:], RT[4][:], ALU.mult))
                link(v.tensor_tensor(RT[5][:], RT[1][:], RT[3][:], ALU.add))
                v.sem_inc(s_pre, 2)

            def slots():
                ranks(1, RT[5], RT[1][:])
                link(v.tensor_tensor(RT[1][:], RT[1][:], ebase[:], ALU.add))

            def place(j):
                link(v.tensor_tensor(RT[2][:], oh[:, j], RT[1][:], ALU.mult))
                link(v.tensor_reduce(RS[0][:], RT[2][:], AX.X, ALU.add))
                link(v.tensor_tensor(RT[2][:], oh[:, j], RT[5][:], ALU.mult))
                link(v.tensor_reduce(RS[1][:], RT[2][:], AX.X, ALU.add))
                link(v.tensor_tensor(RS[0][:], RS[0][:], dump[:, j], ALU.subtract))
                link(v.tensor_tensor(RS[0][:], RS[0][:], RS[1][:], ALU.mult))
                link(v.tensor_tensor(dst_i[:, j], RS[0][:], dump[:, j], ALU.add))
                v.sem_inc(s_ix, 1)

            softmax()
            for grp in range(POOL_LO):
                for c in range(IC):
                    search = search_at(grp, chunk=c)
                    if search:
                        search_count()
                    gated(grp * IC + c, c % 2, c, 0, GN)
                    if search:
                        search_take()
                    if grp == 0 and c < 2:
                        (first_choice, second_choice)[c]()
                for t in range(GT):
                    add_shared(grp * GT + t, t % 2, grp * GT + t)
                    if search_at(grp, tile=t):
                        search_count()
                        search_take()
            masks()
            for grp in range(POOL_LO, SH):
                for c in range(IC):
                    gated(grp * IC + c, c % 2, c, 0, GN, lo=True)
                    if grp == POOL_LO:
                        if c == 0:
                            keep()
                        elif c == 2:
                            slots()
                        elif c == 3:
                            place(0)
                        elif c == 4:
                            place(1)
                for t in range(GT):
                    add_shared(grp * GT + t, t % 2, grp * GT + t)

            def slot_info(e):
                p = e.parity
                dve.wait_ge(s_xg[p], e.pair * 16 + 16)
                dve.wait_ge(s_add[p], e.pair * ADDED + 16)
                v.tensor_copy(wslot[:, p], xg[:, p, :, bass.ds(e.v + DW, 1)].rearrange(
                    "p t o -> p (t o)")).then_inc(s_info, 1)
                v.tensor_scalar(unused[:], xg[:, p, :, RW - 1], 0.0, None, ALU.is_equal).then_inc(s_info, 1)
                dve.wait_ge(s_info, e.v * 3 + 2)
                v.tensor_tensor(unused[:], unused[:], spare[:, p], ALU.mult).then_inc(s_unused, 1)
                dve.wait_ge(s_unused, e.v + 1)
                v.tensor_tensor(row_i[:, p], unused[:], xg[:, p, :, RW - 1], ALU.add).then_inc(s_info, 1)

            def turned(e, t):
                p, cols = e.parity, slice(t * 128, (t + 1) * 128)
                bank = turn[(e.const * CT + t) % 2]
                dve.wait_ge(s_xt, e.v * CT + (t + 1))
                v.tensor_copy(xgs[:, p, HI_A:HI_LO_B + 1, cols],
                              bank[:, 0:256].rearrange("p (c n) -> p c n", c=2)).then_inc(s_xhi, 1)
                dve.wait_ge(s_xhi, e.v * CT + (t + 1))
                v.tensor_tensor(xgs[:, p, LO_A, cols], bank[:, 0:128], xgs[:, p, HI_A, cols].bitcast(F32), ALU.subtract)
                v.tensor_tensor(xgs[DB:128, p, HI_LO_B, cols], bank[DB:128, 128:256],
                                xgs[DB:128, p, HI_LO_B, cols].bitcast(F32), ALU.subtract).then_inc(s_xte, 1)

            def expert(e, more):
                for hf in range(2):
                    for c in range(IC):
                        gated(e.v * (2 * IC) + (U_E0 + hf * IC + c), c % 2, c, hf * HALF, HALF, lo=hf == 0)
                        if hf == 1 and c < CT and more:
                            if c == 0:
                                slot_info(e + 1)
                            turned(e + 1, c)
                for t in range(CT):
                    row = ys[:, e.parity, t, :]
                    dve.wait_ge(s_y1, e.v * CT + (t + 1))
                    v.scalar_tensor_tensor(row, down[(e.const * CT + t) % 2][:, D:2 * D],
                                           wslot[:, e.parity, t:t + 1], row, ALU.mult, ALU.add).then_inc(s_ye, 1)

            slot_info(Tile(0))
            for t in range(CT):
                turned(Tile(0), t)
            with dve.Fori(0, NE // 2 - 1) as r:
                expert(Tile(0, r), True)
                expert(Tile(1, r), True)
            expert(Tile(NE - 2), True)
            expert(Tile(NE - 1), False)


_OUT = (NB, L, D)


def kernel(x, L0_tok_dw_w, L0_tok_pw_w, L0_tok_pw_b, L0_tok_ln_g, L0_tok_ln_b, L0_attn_W_attn,
           L0_attn_b_attn, L0_attn_W_proj, L0_attn_b_proj, L0_ffn_Wr, L0_ffn_w1, L0_ffn_w3, L0_ffn_w2,
           L0_ffn_s1, L0_ffn_s3, L0_ffn_s2):
    import numpy as np
    import concourse.bacc as bacc
    from concourse.bass_utils import run_bass_kernel_spmd

    def chunks(w):
        w = np.asarray(w)
        return np.ascontiguousarray(np.moveaxis(w.reshape(w.shape[:-2] + (2, DC, w.shape[-1])), -3, -2))

    def inner(w):
        w = np.asarray(w)
        return np.ascontiguousarray(np.moveaxis(w.reshape(w.shape[:-2] + (IC, 128, w.shape[-1])), -3, -2))

    x = np.asarray(x)[..., 0]
    pad = (TAPS - 1) // 2
    xp = np.zeros((NB, L + 2 * pad, D), x.dtype)
    xp[:, pad:pad + L] = x
    wp = np.zeros((4, HG, 32, D), x.dtype)
    wp[:, :, 0:HS] = np.asarray(L0_attn_W_proj).reshape(HG, 4, HS, D).transpose(1, 0, 2, 3)
    arrays = {
        "xT": np.ascontiguousarray(xp.transpose(2, 0, 1).reshape(2, DC, NB, L + 2 * pad).transpose(1, 0, 2, 3)),
        "dw": chunks(np.asarray(L0_tok_dw_w).reshape(D, TAPS)),
        "pwT": chunks(np.asarray(L0_tok_pw_w).T),
        "pw_b": np.asarray(L0_tok_pw_b).reshape(1, D),
        "ln_g": np.asarray(L0_tok_ln_g),
        "ln_b": np.asarray(L0_tok_ln_b),
        "wqkv": chunks(L0_attn_W_attn),
        "b_attn": np.asarray(L0_attn_b_attn).reshape(1, 3 * D),
        "wproj": np.ascontiguousarray(wp.transpose(0, 2, 1, 3).reshape(128, HG, D)),
        "b_proj": np.asarray(L0_attn_b_proj),
        "wr": np.asarray(L0_ffn_Wr),
        "w13": np.stack([np.asarray(L0_ffn_w1), np.asarray(L0_ffn_w3)], -2), "w2": inner(L0_ffn_w2),
        "s13": np.stack([np.asarray(L0_ffn_s1), np.asarray(L0_ffn_s3)], -2), "s2": inner(L0_ffn_s2),
    }
    nc = bacc.Bacc("TRN2", target_bir_lowering=False, num_devices=1)
    ins = [nc.dram_tensor(n, a.shape, mybir.dt.from_np(a.dtype), kind="ExternalInput").ap() for n, a in arrays.items()]
    out = nc.dram_tensor("out", _OUT, F32, kind="ExternalOutput").ap()
    vit_tower(nc, *ins, out)
    r = run_bass_kernel_spmd(nc, [arrays], core_ids=[0])
    return r.results[0]["out"]
```

```python
from contextlib import ExitStack

import concourse.bass as bass
from concourse import mybir

ALU = mybir.AluOpType
ACT = mybir.ActivationFunctionType
AX = mybir.AxisListType
F32 = mybir.dt.float32
F32R = mybir.dt.float32r
BF16 = mybir.dt.bfloat16
I32 = mybir.dt.int32
RADD = bass.bass_isa.ReduceOp.add

NB, L, D = 16, 128, 192
N = NB * L
DC = 96
DA, DB = 128, D - 128
DW = D + DB
HI_A, HI_LO_B, LO_A = range(3)
TAPS = 7
NH, HS = 12, 16
HG = 3
NG = NH // HG
NE, INNER = 8, 768
IC = INNER // 128
RW = DW + NE + 1
CAP = (N * 2 * 5 // 4) // NE
CT = CAP // 128
HALF = CAP // 2
GT = 4
GN = GT * L
NEG = -1.0e30
ACTIVE = range(-4, NB + 2)
FIRST, LAST = 2, 11
BITS = 30


class Tile:

    def __init__(self, const, reg=None):
        self.const, self.reg = const, reg

    def __add__(self, k):
        return Tile(self.const + k, self.reg)

    @property
    def v(self):
        return self.const if self.reg is None else self.reg * 2 + self.const

    @property
    def pair(self):
        return self.const // 2 if self.reg is None else self.reg + self.const // 2

    @property
    def parity(self):
        return self.const % 2

    def inside(self):
        return self.reg is not None or 0 <= self.const < NB

    def after(self, k):
        return self.reg is not None or self.const >= k


def vit_tower(nc, xT, dw, pwT, pw_b, ln_g, ln_b, wqkv, b_attn, wproj, b_proj, wr, w13, w2,
              s13, s2, out):
    with ExitStack() as ctx:
        def sb(name, shape, dt=F32, scope=ctx):
            return scope.enter_context(nc.sbuf_tensor(name, shape, dt))

        def ps(name, shape, dt=F32):
            return ctx.enter_context(nc.psum_tensor(name, shape, dt))

        def sem(name):
            return ctx.enter_context(nc.semaphore(name))

        slots_in = nc.dram_tensor("slots_in", [NE * CAP + 2 * N, RW], F32).ap()
        acc = nc.dram_tensor("acc", [1 + N + 2 * CAP, D], F32).ap()

        wr_raw = sb("wr_raw", [128, 2, NE])
        wr_sp = sb("wr_sp", [128, 4, 128], F32R)
        ident = sb("ident", [128, 128])
        tri = sb("tri", [128, 128])
        ones = sb("ones", [128, 128])
        H = sb("H", [128, NB, D])
        xn2 = sb("xn2", [128, NB, RW])
        xs = sb("xs", [128, 3, N], F32R)
        edesc = sb("edesc", [128, NB, NE])
        ebase = sb("ebase", [128, NB, NE])
        dump = sb("dump", [128, 2, NB])
        rt = sb("rt", [128, 8, NB, NE])
        RT = [rt[:, i] for i in range(8)]
        RS = [sb(f"rs{i}", [128, NB]) for i in range(4)]
        score = sb("score", [128, NB, NE])
        oh = sb("oh", [128, 2, NB, NE])
        wgt = sb("wgt", [128, 2, NB])
        thr = sb("thr", [128, NE], I32)
        digit = sb("digit", [128, 3, NE], I32)
        cand = sb("cand", [128, 3, NE], I32)
        above = rt[:, 3:6]
        cnt = sb("cnt", [128, 3, NE])
        tot = sb("tot", [128, 3, NE])
        reach = sb("reach", [128, 3, NE])
        two = sb("two", [128, NE], I32)
        dst_i = sb("dst_i", [128, 2, NB], I32)
        spare = sb("spare", [128, 2, CT])
        unused = sb("unused", [128, CT])
        wslot = sb("wslot", [128, 2, CT])
        row_i = sb("row_i", [128, 2, CT], I32)
        segm = sb("segm", [128, NE, NB])
        raw_a = sb("raw_a", [128, 2, INNER])
        raw_b = sb("raw_b", [128, 2, INNER])
        raw_2 = sb("raw_2", [128, IC, D])
        wa = sb("wa", [128, 2, 2, 2, INNER], F32R)
        wb_hi = sb("wb_hi", [128, 2, 2, INNER], F32R)
        wb_lo = sb("wb_lo", [DB, 2, 2, INNER], F32R)
        w2s = sb("w2s", [128, 2, IC, 2, D], F32R)
        ctx_a = ExitStack()

        def sa(name, shape, dt=F32):
            return sb(name, shape, dt, ctx_a)

        xb = sa("xb", [DC, 2, 2, L + TAPS - 1])
        dw_sb = sa("dw_sb", [DC, 2, TAPS])
        cv = sa("cv", [DC + 1, 2, 2, L])
        pw_sb = sa("pw_sb", [DC + 1, 2, D])
        g_bc = sa("g_bc", [128, D])
        b_bc = sa("b_bc", [128, D])
        bproj_bc = sa("bproj_bc", [128, D])
        wqkv_sb = sa("wqkv_sb", [DC + 1, 2, 3 * D])
        wproj_sb = sa("wproj_sb", [128, HG, D])
        identb = sa("identb", [128, 128], BF16)
        causal = sa("causal", [128, HG, L], BF16)
        headmask = sa("headmask", [DC, 6])
        eps1 = sa("eps1", [128, 1])
        eps2 = sa("eps2", [128, 1])
        mhalf = sa("mhalf", [128, 1])
        st = sa("st", [128, 3, 6])
        mv = sa("mv", [128, 3, 2])
        ve = sa("ve", [128, 3, 1])
        rstd = sa("rstd", [128, 3, 1])
        carry = sa("carry", [128, 3])
        tn = sa("tn", [128, D])
        un = sa("un", [128, D])
        h1 = sa("h1", [128, D])
        xn = sa("xn", [128, D])
        xnT = sa("xnT", [DC + 1, 2, L])
        qT = sa("qT", [DC, 2, L])
        kT = sa("kT", [DC, 2, L])
        kbd = sa("kbd", [DC, 2, 6, L])
        vs = sa("vs", [128, 2, NH, 32])
        probs = sa("probs", [128, NG, HG, L])
        nmax = sa("nmax", [128, NH])
        rsum = sa("rsum", [128, NH])
        rinv = sa("rinv", [128, NH])
        pT = sa("pT", [128, NH, L])
        oT = sa("oT", [128, HG, L])
        hrow = sa("hrow", [128, D])
        xn2s = sa("xn2s", [128, DW])
        ctx_a.close()
        sgf = sb("sgf", [128, 2, 2, GN])
        sg, gf = sgf[:, 0], sgf[:, 1]
        lgT = sgf[0:NE].rearrange("p a b n -> p (a b n)")
        G = sb("G", [128, 2, IC, CAP], F32R)
        xgs = sb("xgs", [128, 2, 3, CAP], F32R)
        ys = sb("ys", [128, 2, CT, D])
        flat_xn2 = xn2[:].rearrange("p t d -> p (t d)")
        xg = flat_xn2[:, 0:2 * CT * RW].rearrange("p (q t d) -> p q t d", q=2, t=CT)

        bank_qv = ps("bank_qv", [128, 512])
        bank_k = ps("bank_k", [128, 512])
        bank_s = [ps(f"bank_s{g}", [128, 512]) for g in range(NG)]
        bank_o = ps("bank_o", [128, 512])
        bank_y = ps("bank_y", [128, 512])
        up_a, up_b = bank_s[0:2], bank_s[2:4]
        down = [bank_o, bank_y]
        turn = [bank_qv, bank_k]

        s_x = [sem("s_x0"), sem("s_x1")]
        s_dw = sem("s_dw")
        s_wa = sem("s_wa")
        s_bc = sem("s_bc")
        s_cst = sem("s_cst")
        s_cd = sem("s_cd")
        s_pc = sem("s_pc")
        s_tap0 = sem("s_tap0")
        s_conv = sem("s_conv")
        s_y = sem("s_y")
        s_ln = sem("s_ln")
        s_r1 = sem("s_r1")
        s_r2 = sem("s_r2")
        s_r3 = sem("s_r3")
        s_relu = sem("s_relu")
        s_h1b = sem("s_h1b")
        s_t1 = sem("s_t1")
        s_xnt = sem("s_xnt")
        s_k = sem("s_k")
        s_qvm = sem("s_qvm")
        s_qv = sem("s_qv")
        s_kt = sem("s_kt")
        s_kbd = sem("s_kbd")
        s_s = sem("s_s")
        s_max = sem("s_max")
        s_exp = sem("s_exp")
        s_rinv = sem("s_rinv")
        s_norm = sem("s_norm")
        s_ptm = sem("s_ptm")
        s_pt = sem("s_pt")
        s_pv = sem("s_pv")
        s_o = sem("s_o")
        s_proj = sem("s_proj")
        s_l3 = sem("s_l3")
        s_t2 = sem("s_t2")
        s_xn2t = sem("s_xn2t")
        s_xlo = sem("s_xlo")
        s_raw = [sem(f"s_raw{i}") for i in range(3)]
        s_hiw = sem("s_hiw")
        s_low = sem("s_low")
        s_hi = sem("s_hi")
        s_lo = sem("s_lo")
        s_hc = sem("s_hc")
        s_wrs = sem("s_wrs")
        s_zero = sem("s_zero")
        s_zf = sem("s_zf")
        s_lg = sem("s_lg")
        s_lgc = sem("s_lgc")
        s_lgt = sem("s_lgt")
        s_rt = sem("s_rt")
        s_rex = sem("s_rex")
        s_thr = sem("s_thr")
        s_cnt = sem("s_cnt")
        s_tot = sem("s_tot")
        s_pre = sem("s_pre")
        s_ix = sem("s_ix")
        s_scat = sem("s_scat")
        s_sw = sem("s_sw")
        s_xg = [sem("s_xg0"), sem("s_xg1")]
        s_u = sem("s_u")
        s_silu = sem("s_silu")
        s_mul = sem("s_mul")
        s_d = sem("s_d")
        s_ye = sem("s_ye")
        s_xt = sem("s_xt")
        s_xte = sem("s_xte")
        s_xhi = sem("s_xhi")
        s_add = [sem("s_add0"), sem("s_add1")]
        s_info = sem("s_info")
        s_sh = sem("s_sh")
        s_y1 = sem("s_y1")
        s_unused = sem("s_unused")
        s_wt = sem("s_wt")
        s_base = sem("s_base")
        s_out = sem("s_out")

        N_ZERO = -(-NE * CAP * RW // 128 // (2 * CT * D))
        N_WA = 5
        TAP_OPS = 2 * (TAPS - 1)
        FREE = 2
        ADDED = 16 * CT
        SH = NB // GT
        PLACE = 1
        HELP = PLACE + 1
        HI_AT = 3
        PIECES = 11
        EARLY = 5
        TURN_AT = ((0, 1), (2,), (3, 4), (), ())
        U_E0, D_E0 = SH * IC, SH * GT

        def search_at(grp, chunk=None, tile=None):
            if grp == 0:
                return tile is not None or chunk >= 2
            return grp == 1 and chunk is not None

        def steps(eng, body):
            for i in ACTIVE:
                if i < FIRST or i > LAST:
                    body(Tile(i))
                elif i == FIRST:
                    with eng.Fori(0, (LAST - FIRST + 1) // 2) as r:
                        body(Tile(FIRST, r))
                        body(Tile(FIRST + 1, r))

        block = ctx.enter_context(nc.Block())

        @block.sync
        def _(sp):
            def load_x(b):
                if b.after(2):
                    sp.wait_ge(s_conv, b.v * TAP_OPS - TAP_OPS)
                sp.dma_start(xb[:, b.parity, :, :], xT[:, :, bass.ds(b.v, 1), :].rearrange(
                    "p c o n -> p c (o n)")).then_inc(s_x[b.parity], 16)

            load_x(Tile(0))
            sp.dma_start(dw_sb[:], dw).then_inc(s_dw, 16)
            load_x(Tile(1))
            sp.dma_start(pw_sb[0:DC], pwT).then_inc(s_wa, 16)
            sp.dma_start(pw_sb[DC:DC + 1, 1, :], pw_b).then_inc(s_wa, 16)
            sp.dma_start(g_bc[:], ln_g.partition_broadcast(128)).then_inc(s_bc, 16)
            sp.dma_start(b_bc[:], ln_b.partition_broadcast(128)).then_inc(s_bc, 16)
            sp.dma_start(wqkv_sb[0:DC], wqkv).then_inc(s_wa, 16)
            sp.dma_start(wqkv_sb[DC:DC + 1, 1, :], b_attn).then_inc(s_wa, 16)
            sp.dma_start(bproj_bc[:], b_proj.partition_broadcast(128)).then_inc(s_bc, 16)
            sp.dma_start(wproj_sb[:], wproj).then_inc(s_wa, 16)
            sp.dma_start(wr_raw[:, 0], wr[0:DA]).then_inc(s_sw, 16)
            for half in (wr_raw[0:DB, 1], wr_raw[DB:128, 1]):
                sp.dma_start(half, wr[DA:D]).then_inc(s_sw, 16)

            def load_w(gate_up, w_down, hi=None, low=None):
                if low is not None:
                    sp.wait_ge(s_hiw, hi)
                    sp.wait_ge(s_low, low(4))
                sp.dma_start(raw_a[:], gate_up[0:DA]).then_inc(s_raw[0], 16)
                if low is not None:
                    sp.wait_ge(s_low, low(8))
                sp.dma_start(raw_b[0:DB], gate_up[DA:D]).then_inc(s_raw[1], 16)
                sp.dma_start(raw_b[DB:128], gate_up[DA:D]).then_inc(s_raw[1], 16)
                if low is not None:
                    sp.wait_ge(s_low, low(PIECES))
                sp.dma_start(raw_2[:], w_down).then_inc(s_raw[2], 16)

            for b in range(2, NB):
                load_x(Tile(b))
            load_w(s13, s2)

            def load_expert(e):
                load_w(w13[bass.ds(e.v, 1)].rearrange("o p w n -> p (o w) n"),
                       w2[bass.ds(e.v, 1)].rearrange("o p c n -> p (o c) n"),
                       e.v * 3 + 3, lambda n: e.v * PIECES + n)

            load_expert(Tile(0))
            sp.wait_ge(s_zf, 1)
            zeros = ys[:].rearrange("p e c d -> p (e c d)")
            per = NE * CAP * RW // 128
            share = slots_in[0:NE * CAP, :].rearrange("(p n) d -> p (n d)", p=128)
            step = 2 * CT * D
            for c in range(0, per, step):
                n = min(step, per - c)
                sp.dma_start(share[:, c:c + n], zeros[:, 0:n]).then_inc(s_zero, 16)
            load_expert(Tile(1))

            def store_base(grp):
                sp.wait_ge(s_ye, GT * (grp + 1) + FREE)
                sp.dma_start(acc[1 + grp * GN:1 + (grp + 1) * GN, :].rearrange("(t p) d -> p t d", p=128),
                             H[:, grp * GT:(grp + 1) * GT, :]).then_inc(s_base, 16)

            for grp in range(HELP):
                store_base(grp)

            def load_xg(e):
                sp.dma_start(xg[:, e.parity], slots_in[bass.ds(e.v * CAP, CAP), :].rearrange(
                    "(t p) d -> p t d", p=128)).then_inc(s_xg[e.parity], 16)

            sp.wait_ge(s_scat, 16 * 2 * NB)
            load_xg(Tile(0))
            load_xg(Tile(1))
            for grp in range(HELP, SH):
                store_base(grp)

            def expert(e):
                sp.wait_ge(s_xt, e.v * CT + CT)
                sp.wait_ge(s_info, e.v * 3 + 3)
                load_xg(e + 2)
                load_expert(e + 2)

            with sp.Fori(0, NE // 2 - 1) as r:
                expert(Tile(0, r))
                expert(Tile(1, r))
            for p in range(2):
                sp.wait_ge(s_add[p], ADDED * (NE // 2) + 16)
            sp.dma_start(out.rearrange("b n d -> (b n) d"), acc[1:1 + N, :]).then_inc(s_out, 16)
            sp.wait_ge(s_out, 16)

        @block.gpsimd
        def _(pool):
            g = nc.gpsimd
            g.memset(ident[:], 0.0).then_inc(s_pc, 1)
            g.memset(causal[:], 0.0).then_inc(s_pc, 1)
            g.memset(headmask[:], 1.0).then_inc(s_pc, 1)
            g.memset(tri[:], 1.0).then_inc(s_pc, 1)
            g.memset(ones[:], 1.0)
            g.memset(eps1[:], 1e-6)
            g.memset(eps2[:], 1e-5)
            g.memset(mhalf[:], -0.5)
            g.memset(segm[:], 1.0).then_inc(s_pc, 1)
            pool.sem_inc(s_lo, FREE)
            pool.wait_ge(s_pc, 5)
            g.affine_select(out=ident[:], in_=ident[:], compare_op=ALU.not_equal, fill=1.0, base=0,
                            pattern=[[-1, 128]], channel_multiplier=1).then_inc(s_pc, 1)
            g.affine_select(out=causal[:], in_=causal[:], compare_op=ALU.is_ge, fill=NEG, base=0,
                            pattern=[[0, HG], [-1, L]], channel_multiplier=1)
            g.affine_select(out=headmask[:], in_=headmask[:], compare_op=ALU.is_ge, fill=0.0, base=0,
                            pattern=[[-HS, 6]], channel_multiplier=1).then_inc(s_pc, 1)
            g.affine_select(out=tri[:], in_=tri[:], compare_op=ALU.is_gt, fill=0.0, base=0,
                            pattern=[[1, 128]], channel_multiplier=-1)
            g.affine_select(out=segm[:], in_=segm[:], compare_op=ALU.is_gt, fill=0.0, base=0,
                            pattern=[[0, NE], [1, NB]], channel_multiplier=0)
            pool.wait_ge(s_pc, 7)
            g.affine_select(out=headmask[:], in_=headmask[:], compare_op=ALU.is_ge, fill=0.0, base=HS - 1,
                            pattern=[[HS, 6]], channel_multiplier=-1)
            g.tensor_copy(identb[:], ident[:])
            g.iota(edesc[:], pattern=[[0, NB], [-1, NE]], base=NE, channel_multiplier=0,
                   allow_small_or_imprecise_dtypes=True)
            g.iota(ebase[:], pattern=[[0, NB], [CAP, NE]], base=0, channel_multiplier=0,
                   allow_small_or_imprecise_dtypes=True)
            g.iota(xn2[:, :, RW - 1], pattern=[[L, NB]], base=1, channel_multiplier=1,
                   allow_small_or_imprecise_dtypes=True)
            g.iota(spare[:], pattern=[[CAP, 2], [128, CT]], base=1 + N, channel_multiplier=1,
                   allow_small_or_imprecise_dtypes=True)
            g.iota(dump[:], pattern=[[N, 2], [L, NB]], base=NE * CAP, channel_multiplier=1,
                   allow_small_or_imprecise_dtypes=True).then_inc(s_cst, 1)
            pool.wait_ge(s_bc, 16 * 3)

            def rsqrt(n, eps, done, b, stats):
                pool.wait_ge(s_l3 if n == 2 else s_ln, stats)
                g.tensor_tensor(ve[:, n], mv[:, n, 1:2], eps[:], ALU.add).then_inc(done, 1)
                pool.wait_ge(done, b.v * 2 + 1)
                g.tensor_tensor(rstd[:, n], ve[:, n], mhalf[:], ALU.pow).then_inc(done, 1)

            def split_lo(job, par, n):
                m, k = (n // 4, n % 4) if n < 8 else (2, n - 8)
                half, cols = k // 2, slice(k % 2 * (INNER // 2), (k % 2 + 1) * (INNER // 2))
                if m == 0:
                    lo, raw, hi = wa[:, par, 1, half, cols], raw_a[:, half, cols], wa[:, par, 0, half, cols]
                elif m == 1:
                    lo, raw, hi = wb_lo[:, par, half, cols], raw_b[0:DB, half, cols], wb_hi[0:DB, par, half, cols]
                else:
                    pair = slice(2 * k, 2 * k + 2)
                    lo, raw, hi = w2s[:, par, pair, 1], raw_2[:, pair], w2s[:, par, pair, 0]
                pool.wait_ge(s_hiw, job * 3 + (m + 1))
                g.tensor_tensor(lo, raw, hi.bitcast(F32), ALU.subtract).then_inc(s_low, 1)

            def g_lo(u, par, c, c0, n):
                pool.wait_ge(s_hi, u + 1)
                g.tensor_tensor(G[:, 1, c, c0:c0 + n], gf[:, par, 0:n], G[:, 0, c, c0:c0 + n].bitcast(F32),
                                ALU.subtract).then_inc(s_lo, 1)

            def norm(b, k):
                pool.wait_ge(s_rinv, b.v * NG + (k + 1))
                g.tensor_tensor(probs[:, k], probs[:, k],
                                rinv[:, HG * k:HG * (k + 1)].unsqueeze(2).to_broadcast([128, HG, L]),
                                ALU.mult).then_inc(s_norm, 1)

            def keys(b):
                pool.wait_ge(s_kt, b.v + 1)
                if b.after(1):
                    pool.wait_ge(s_s, b.v * NG)
                g.tensor_tensor(kbd[:, 1], kT[:, 1].unsqueeze(1).to_broadcast([DC, 6, L]),
                                headmask[:].unsqueeze(2).to_broadcast([DC, 6, L]), ALU.mult).then_inc(s_kbd, 1)

            def step(i):
                b = i
                if b.inside():
                    norm(b, 0)
                n = i + 2
                if n.inside():
                    rsqrt(0, eps1, s_r1, n, n.v * 7 + 2)
                if b.inside():
                    norm(b, 1)
                    norm(b, 2)
                    norm(b, 3)
                m = i + -1
                if m.inside():
                    rsqrt(2, eps2, s_r3, m, m.v * 5 + 3)
                if (i + 1).inside():
                    keys(i + 1)
                if n.inside():
                    rsqrt(1, eps2, s_r2, n, n.v * 7 + 6)
                if n.inside():
                    pool.wait_ge(s_relu, n.v + 1)
                    g.tensor_tensor(H[:, bass.ds(n.v, 1)].rearrange("p o d -> p (o d)"), h1[:], bproj_bc[:],
                                    ALU.add).then_inc(s_h1b, 1)
                if i.reg is None:
                    for n in {LAST + 2: (0, 1), LAST + 3: (2, 3), LAST + 4: (4, 5, 6, 7),
                              LAST + 5: (8, 9, 10)}.get(i.const, ()):
                        split_lo(0, 0, n)

            steps(pool, step)

            pool.wait_ge(s_proj, NB)
            pool.wait_ge(s_hc, NB)
            g.memset(ys[:].rearrange("p e t d -> p (e t d)"), 0.0).then_inc(s_zf, 1)
            pool.wait_ge(s_zf, 1)
            for p in range(2):
                pool.dma_start(acc[1 + N + p * CAP:1 + N + (p + 1) * CAP, :].rearrange("(t p) d -> p t d", p=128),
                               ys[:, p]).then_inc(s_add[p], 16)
            done = 0

            def all_sums():
                nonlocal done
                done += 1
                pool.wait_ge(s_cnt, done)
                g.partition_all_reduce(tot[:].rearrange("p k e -> p (k e)"), cnt[:].rearrange("p k e -> p (k e)"),
                                       128, RADD).then_inc(s_tot, 1)

            pieces = list(range(PIECES))
            for grp in range(HELP):
                for c in range(IC):
                    if search_at(grp, chunk=c):
                        all_sums()
                    g_lo(grp * IC + c, c % 2, c, 0, GN)
                for t in range(-1, GT):
                    if search_at(grp, tile=t):
                        all_sums()
                        split_lo(1, 1, pieces.pop(0))
                if grp == PLACE:
                    all_sums()
                    for n in pieces:
                        split_lo(1, 1, n)

            pool.wait_ge(s_zero, 16 * N_ZERO)
            pool.wait_ge(s_hc, NB)
            pool.wait_ge(s_wt, 1)
            for j in range(2):
                pool.wait_ge(s_ix, j + 1)
                for t in range(NB):
                    pool.indirect_dma_start(slots_in, bass.IndirectOffsetOnAxis(ap=dst_i[:, j, t:t + 1], axis=0),
                                            xn2[:, t, :], None).then_inc(s_scat, 16)

            def rows_ready(e, t):
                if t == 1:
                    before = e.pair if e.parity == 0 else e.pair + 1
                    pool.wait_ge(s_add[1 - e.parity], before * ADDED + 16)
                pool.wait_ge(s_ye, e.v * CT + (D_E0 + t + 1 + FREE))

            def add_rows(e, t):
                pool.indirect_dma_start(acc, bass.IndirectOffsetOnAxis(ap=row_i[:, e.parity, t:t + 1], axis=0),
                                        ys[:, e.parity, t, :], None, compute_op=ALU.add,
                                        ).then_inc(s_add[e.parity], 16)

            def expert(e, more):
                for c in range(IC):
                    g_lo(e.v * (2 * IC) + (U_E0 + IC + c), c % 2, c, HALF, HALF)
                    if 1 <= c <= EARLY and more:
                        split_lo(e.v + 2, e.parity, c - 1)
                if more:
                    for n in range(EARLY, PIECES - CT + 1):
                        split_lo(e.v + 2, e.parity, n)
                for t in range(1, CT):
                    rows_ready(e, t)
                    if more:
                        split_lo(e.v + 2, e.parity, PIECES - CT + t)
                    if t == 1:
                        add_rows(e, 0)
                    add_rows(e, t)

            pool.wait_ge(s_base, 16 * SH)
            with pool.Fori(0, NE // 2 - 1) as r:
                expert(Tile(0, r), True)
                expert(Tile(1, r), True)
            expert(Tile(NE - 2), True)
            expert(Tile(NE - 1), False)

        @block.scalar
        def _(act):
            s = nc.scalar

            def exp(b, k):
                act.wait_ge(s_max, b.v * NG + (k + 1))
                if b.after(1):
                    act.wait_ge(s_ptm, b.v * NG + (k + 1 - NG))
                for h in range(HG):
                    c = HG * k + h
                    last = s.activation(probs[:, k, h], bank_s[k][:, h * L:(h + 1) * L], ACT.Exp,
                                        bias=nmax[:, c:c + 1], accum_out=rsum[:, c:c + 1])
                last.then_inc(s_exp, 1)

            def evac_qv(b):
                act.wait_ge(s_qvm, b.v + 1)
                if b.after(1):
                    act.wait_ge(s_s, b.v * NG)
                s.activation(qT[:].rearrange("p c n -> p (c n)"), bank_qv[0:DC, 0:2 * L], ACT.Copy,
                             scale=float(HS) ** -0.5).then_inc(s_qv, 1)
                if b.after(2):
                    act.wait_ge(s_pv, b.v - 1)
                s.activation(vs[:, b.parity, :, 0:HS], bank_qv[:, 2 * L:2 * L + D].rearrange(
                    "p (h d) -> p h d", h=NH), ACT.Copy).then_inc(s_qv, 1)

            def first_tap(b):
                act.wait_ge(s_x[b.parity], b.pair * 16 + 16)
                if b.after(2):
                    act.wait_ge(s_y, b.v - 1)
                for c in range(2):
                    s.activation(cv[0:DC, b.parity, c], xb[:, b.parity, c, 0:L], ACT.Copy,
                                 scale=dw_sb[:, c, 0:1]).then_inc(s_tap0, 1)

            def evac_k(b):
                act.wait_ge(s_k, b.v + 1)
                if b.after(1):
                    act.wait_ge(s_kbd, b.v * 2)
                s.activation(kT[:].rearrange("p c n -> p (c n)"), bank_k[0:DC, 0:2 * L], ACT.Copy).then_inc(s_kt, 1)

            def relu(b):
                act.wait_ge(s_ln, b.v * 7 + 4)
                if b.after(1):
                    act.wait_ge(s_h1b, b.v)
                s.activation(h1[:], un[:], ACT.Relu).then_inc(s_relu, 1)

            def evac_pt(b, k):
                act.wait_ge(s_ptm, b.v * NG + (k + 1))
                if b.after(1):
                    act.wait_ge(s_pv, b.v)
                s.activation(pT[:, HG * k:HG * (k + 1)].rearrange("p h n -> p (h n)"),
                             bank_s[k][:, 0:HG * L], ACT.Copy).then_inc(s_pt, 1)

            def evac_o(b):
                act.wait_ge(s_pv, b.v + 1)
                if b.after(1):
                    act.wait_ge(s_proj, b.v)
                s.activation(oT[:].rearrange("p h n -> p (h n)"), bank_o[:, 0:HG * L], ACT.Copy).then_inc(s_o, 1)

            def evac_t2(b):
                act.wait_ge(s_t2, b.v + 1)
                s.activation(xs[:, HI_A:HI_LO_B + 1, bass.ds(b.v * L, L)],
                             bank_k[:, 0:2 * L].rearrange("p (c n) -> p c n", c=2), ACT.Copy).then_inc(s_xn2t, 1)

            def copy_rows(b):
                act.wait_ge(s_l3, b.v * 5 + 5)
                s.activation(H[:, bass.ds(b.v, 1)].rearrange("p o d -> p (o d)"), hrow[:], ACT.Copy)
                s.activation(xn2[:, bass.ds(b.v, 1), 0:DW].rearrange("p o d -> p (o d)"), xn2s[:], ACT.Copy).then_inc(s_hc, 1)

            def evac_t1(b):
                act.wait_ge(s_t1, b.v + 1)
                if b.after(1):
                    act.wait_ge(s_qvm, b.v)
                s.activation(xnT[0:DC].rearrange("p c n -> p (c n)"), bank_qv[0:DC, 0:2 * L],
                             ACT.Copy).then_inc(s_xnt, 1)

            def step(i):
                if (i + 4).inside():
                    first_tap(i + 4)
                if i.inside():
                    exp(i, 0)
                if (i + -2).inside():
                    evac_t2(i + -2)
                if (i + 1).inside():
                    evac_t1(i + 1)
                if i.inside():
                    for k in range(1, NG - 1):
                        exp(i, k)
                if (i + 1).inside():
                    evac_k(i + 1)
                if i.inside():
                    exp(i, NG - 1)
                if (i + 1).inside():
                    evac_qv(i + 1)
                if (i + 2).inside():
                    relu(i + 2)
                if i.inside():
                    for k in range(NG):
                        evac_pt(i, k)
                    evac_o(i)
                if (i + -1).inside():
                    copy_rows(i + -1)
                if i.reg is None and i.const == NB - 1:
                    for grp in range(SH - 1):
                        evac_logits(grp)
                if i.reg is None and LAST < i.const <= LAST + 3:
                    split_hi(0, 0, i.const - LAST - 1)

            def evac_logits(grp):
                act.wait_ge(s_lg, grp + 1)
                s.activation(lgT[:, grp * GN:(grp + 1) * GN], bank_s[grp][0:NE, 0:GN], ACT.Copy).then_inc(s_lgc, 1)

            def split_hi(job, par=0, n=None):
                for k, (hi, raw) in enumerate(((wa[:, par, 0], raw_a[:]), (wb_hi[:, par], raw_b[:]),
                                               (w2s[:, par, :, 0], raw_2[:]))):
                    if n is None or k == n:
                        loads = 32 if k == 1 else 16
                        act.wait_ge(s_raw[k], job * loads + loads)
                        s.activation(hi, raw, ACT.Copy).then_inc(s_hiw, 1)

            act.wait_ge(s_cd, 4)
            act.wait_ge(s_dw, 16)
            steps(act, step)

            evac_logits(SH - 1)
            act.wait_ge(s_rt, 2)
            s.activation(RT[1][:], RT[1][:], ACT.Exp).then_inc(s_rex, 1)

            def silu(u, u_par, n):
                act.wait_ge(s_u, u + 1)
                act.wait_ge(s_mul, u + 1)
                s.activation(sg[:, u_par, 0:n], up_a[u_par][:, 0:n], ACT.Silu).then_inc(s_silu, 1)

            def g_hi(u, par, c):
                act.wait_ge(s_mul, u + (FREE + 1))
                s.activation(G[:, 0, c, 0:GN], gf[:, par, 0:GN], ACT.Copy).then_inc(s_hi, 1)

            for grp in range(SH):
                for c in range(IC):
                    u = grp * IC + c
                    silu(u, c % 2, GN)
                    if grp < HELP and c >= 1:
                        g_hi(u - 1, (c - 1) % 2, c - 1)
                    if grp == 0 and 1 <= c < 4:
                        split_hi(1, 1, c - 1)
                if grp < HELP:
                    g_hi(grp * IC + IC - 1, (IC - 1) % 2, IC - 1)

            def expert(e, more):
                for hf in range(2):
                    for c in range(IC):
                        silu(e.v * (2 * IC) + (U_E0 + hf * IC + c), c % 2, HALF)
                        if hf == 0 and c == 3 and more:
                            act.wait_ge(s_d, e.v * CT + D_E0)
                        if HI_AT <= hf * IC + c < HI_AT + 3 and more:
                            split_hi(e.v + 2, e.parity, hf * IC + c - HI_AT)
                for t in range(CT):
                    if t == 0:
                        act.wait_ge(s_add[e.parity], e.pair * ADDED + 16)
                        act.wait_ge(s_info, e.v * 3 + 3)
                    act.wait_ge(s_d, e.v * CT + (D_E0 + t + 1))
                    s.activation(ys[:, e.parity, t, :], down[(e.const * CT + t) % 2][:, 0:D],
                                 ACT.Copy, scale=wslot[:, e.parity, t:t + 1]).then_inc(s_y1, 1)

            act.wait_ge(s_zero, 16 * N_ZERO)
            for p in range(2):
                act.wait_ge(s_add[p], 16)
            with act.Fori(0, NE // 2 - 1) as r:
                expert(Tile(0, r), True)
                expert(Tile(1, r), True)
            expert(Tile(NE - 2), True)
            expert(Tile(NE - 1), False)

        @block.tensor
        def _(pe):
            mm = nc.tensor.matmul

            def rows(c):
                return slice(0, DC + c)

            def pointwise(b):
                pe.wait_ge(s_conv, b.v * TAP_OPS + TAP_OPS)
                if b.after(1):
                    pe.wait_ge(s_ln, b.v * 7 - 4)
                for c in range(2):
                    last = mm(bank_y[:, 0:D], cv[rows(c), b.parity, c], pw_sb[rows(c), c], start=c == 0, stop=c == 1)
                last.then_inc(s_y, 1)

            def turn_xn(b):
                pe.wait_ge(s_ln, b.v * 7 + 7)
                if b.after(1):
                    pe.wait_ge(s_qv, b.v * 2)
                for c in range(2):
                    last = nc.tensor.transpose(bank_qv[0:DC, c * L:(c + 1) * L], xn[:, c * DC:(c + 1) * DC], ident[:])
                last.then_inc(s_t1, 1)

            def qkv(b):
                pe.wait_ge(s_xnt, b.v + 1)
                if b.after(3):
                    pe.wait_ge(s_xlo, b.v * 2 - 4)
                if b.after(1):
                    pe.wait_ge(s_kt, b.v)
                for m in range(2):
                    for c in range(2):
                        last = mm(bank_k[0:DC, m * L:(m + 1) * L], wqkv_sb[rows(c), c, D + m * DC:D + (m + 1) * DC],
                                  xnT[rows(c), c], start=c == 0, stop=c == 1)
                last.then_inc(s_k, 1)
                for m in range(2):
                    for c in range(2):
                        mm(bank_qv[0:DC, m * L:(m + 1) * L], wqkv_sb[rows(c), c, m * DC:(m + 1) * DC],
                           xnT[rows(c), c], start=c == 0, stop=c == 1)
                for c in range(2):
                    last = mm(bank_qv[:, 2 * L:2 * L + D], xnT[rows(c), c], wqkv_sb[rows(c), c, 2 * D:3 * D],
                              start=c == 0, stop=c == 1)
                last.then_inc(s_qvm, 1)

            def scores(b, banks):
                if banks[0] == 0:
                    pe.wait_ge(s_qv, b.v * 2 + 1)
                    pe.wait_ge(s_kbd, b.v * 2 + 2)
                for k in banks:
                    if b.after(1):
                        pe.wait_ge(s_pt, b.v * NG + (k + 1 - NG))
                    m, h0 = k // 2, HG * (k % 2)
                    mm(bank_s[k][:, 0:HG * L], qT[:, m], kbd[:, m, h0:h0 + HG].rearrange("p h n -> p (h n)"),
                       start=True, stop=False)
                    mm(bank_s[k][:, 0:HG * L], identb[:], causal[:].rearrange("p h n -> p (h n)"),
                       start=False, stop=True).then_inc(s_s, 1)

            def turn_p(b):
                for k in range(NG):
                    pe.wait_ge(s_norm, b.v * NG + (k + 1))
                    for h in range(HG):
                        last = nc.tensor.transpose(bank_s[k][:, h * L:(h + 1) * L], probs[:, k, h], ident[:])
                    last.then_inc(s_ptm, 1)

            def pv(b):
                pe.wait_ge(s_qv, b.v * 2 + 2)
                pe.wait_ge(s_pt, b.v * NG + NG)
                if b.after(1):
                    pe.wait_ge(s_l3, b.v * 5 - 4)
                for h in range(NH):
                    j, q = h // 4, h % 4
                    last = mm(bank_o[32 * q:32 * q + 32, j * L:(j + 1) * L], vs[:, b.parity, h], pT[:, h],
                              start=True, stop=True)
                last.then_inc(s_pv, 1)

            def project(b):
                pe.wait_ge(s_o, b.v + 1)
                for j in range(HG):
                    last = mm(bank_o[:, 0:D], oT[:, j], wproj_sb[:, j], start=j == 0, stop=j == HG - 1)
                last.then_inc(s_proj, 1)

            def turn_xn2(b):
                pe.wait_ge(s_l3, b.v * 5 + 5)
                if b.reg is not None or b.const + 2 < NB:
                    pe.wait_ge(s_kt, b.v + 3)
                if b.after(1):
                    pe.wait_ge(s_xlo, b.v * 2)
                for c in range(2):
                    last = nc.tensor.transpose(bank_k[:, c * L:(c + 1) * L], xn2s[:, c * DA:(c + 1) * DA], ident[:])
                last.then_inc(s_t2, 1)

            def split_product(bank, w, x):
                hi_a, lo_a, hi_b, lo_b = w
                mm(bank, hi_a, x(HI_A), start=True, stop=False)
                mm(bank, hi_a, x(LO_A), start=False, stop=False)
                mm(bank, lo_a, x(HI_A), start=False, stop=False)
                mm(bank, hi_b, x(HI_LO_B), start=False, stop=False)
                return mm(bank, lo_b, x(HI_LO_B, DB), start=False, stop=True)

            def tokens(c0):
                return lambda part, rows=128: xs[0:rows, part, bass.ds(c0, GN)]

            def logits(grp):
                if grp == 0:
                    pe.wait_ge(s_wrs, 5)
                pe.wait_ge(s_xlo, 2 * GT * (grp + 1))
                split_product(bank_s[grp][:, 0:GN], (wr_sp[:, 0], wr_sp[:, 2], wr_sp[:, 1], wr_sp[0:DB, 3]),
                              tokens(GN * grp)).then_inc(s_lg, 1)

            def step(i):
                if i.inside():
                    scores(i, (0, 1))
                if (i + -2).inside():
                    turn_xn2(i + -2)
                if (i + 1).inside():
                    turn_xn(i + 1)
                if i.inside():
                    scores(i, (2, 3))
                if (i + -1).inside():
                    project(i + -1)
                if (i + 1).inside():
                    qkv(i + 1)
                if i.inside():
                    turn_p(i)
                if (i + 3).inside():
                    pointwise(i + 3)
                if i.inside():
                    pv(i)
                if i.reg is None and i.const == NB - 1:
                    for grp in range(SH - 1):
                        logits(grp)

            pe.wait_ge(s_cst, 1)
            pe.wait_ge(s_cd, 4)
            pe.wait_ge(s_wa, 16 * N_WA)
            steps(pe, step)

            logits(SH - 1)
            pe.wait_ge(s_lgc, SH)
            for t in range(NB):
                last = nc.tensor.transpose(turn[0][:, t * NE:(t + 1) * NE], lgT[:, t * L:(t + 1) * L], ident[0:NE, 0:NE])
            last.then_inc(s_lgt, 1)

            def up(u, par, w, c, x, n):
                cs = slice(c * 128, (c + 1) * 128)
                pe.wait_ge(s_mul, u + 1)
                for k, bank in enumerate((up_a, up_b)):
                    last = split_product(bank[par][:, 0:n], (wa[:, w, 0, k, cs], wa[:, w, 1, k, cs],
                                                             wb_hi[:, w, k, cs], wb_lo[:, w, k, cs]), x)
                last.then_inc(s_u, 1)

            def down_tile(d, par, u_done, c0, w, fresh):
                pe.wait_ge(s_ye, d + 1)
                for c in range(IC):
                    if fresh:
                        pe.wait_ge(s_lo, u_done + (FREE + c + 1 - IC))
                    hi, lo = G[:, 0, c, c0:c0 + 128], G[:, 1, c, c0:c0 + 128]
                    mm(down[par][:, 0:2 * D], hi, w2s[:, w, c].rearrange("p h d -> p (h d)"), start=c == 0,
                       stop=False)
                    last = mm(down[par][:, 0:D], lo, w2s[:, w, c, 0], start=False, stop=c == IC - 1)
                last.then_inc(s_d, 1)

            def ranks(n):
                pe.wait_ge(s_pre, 2 * n + 1)
                m = RT[4 + n]
                mm(turn[1][:, 0:NB * NE], tri[:], m[:].rearrange("p t e -> p (t e)"), start=True, stop=True)
                mm(turn[1][:, 128:128 + NB * NE], ones[:], m[:].rearrange("p t e -> p (t e)"),
                   start=True, stop=True).then_inc(s_lgt, 1)

            def turn_slots(e, t):
                if t == 0:
                    pe.wait_ge(s_xg[e.parity], e.pair * 16 + 16)
                if e.reg is not None or e.const * CT + t >= 2:
                    pe.wait_ge(s_xte, e.v * CT + (t - 1))
                for c in range(2):
                    last = nc.tensor.transpose(turn[(e.const * CT + t) % 2][:, c * 128:(c + 1) * 128],
                                               xg[:, e.parity, t, c * DA:(c + 1) * DA], ident[:])
                last.then_inc(s_xt, 1)

            def shared(grp):
                for c in range(IC):
                    up(grp * IC + c, c % 2, 0, c, tokens(grp * GN), GN)
                for t in range(GT):
                    down_tile(grp * GT + t, t % 2, grp * IC + IC, t * 128, 0, t == 0)
                    if grp == PLACE and t < 2:
                        ranks(t)
                    if grp == SH - 1:
                        for n in TURN_AT[t]:
                            turn_slots(Tile(0), n)

            pe.wait_ge(s_low, PIECES)
            for grp in range(SH):
                shared(grp)

            def expert(e, more):
                p, w = e.parity, (e + 1).parity
                pe.wait_ge(s_low, e.v * PIECES + (PIECES + 8))
                pe.wait_ge(s_xte, e.v * CT + CT)
                for hf in range(2):
                    for c in range(IC):
                        up(e.v * (2 * IC) + (U_E0 + hf * IC + c), c % 2, w, c,
                           lambda part, rows=128: xgs[0:rows, p, part, hf * HALF:(hf + 1) * HALF], HALF)
                pe.wait_ge(s_low, e.v * PIECES + 2 * PIECES)
                for t in range(CT):
                    first = (t + 1) * 128 <= HALF
                    u_done = U_E0 + (IC if first else 2 * IC)
                    down_tile(e.v * CT + (D_E0 + t), (e.const * CT + t) % 2, e.v * (2 * IC) + u_done, t * 128, w,
                              t == (0 if first else HALF // 128))
                    if more:
                        for n in TURN_AT[t]:
                            turn_slots(e + 1, n)

            with pe.Fori(0, NE // 2 - 1) as r:
                expert(Tile(0, r), True)
                expert(Tile(1, r), True)
            expert(Tile(NE - 2), True)
            expert(Tile(NE - 1), False)

        @block.vector
        def _(dve):
            v = nc.vector
            v.memset(cv[DC:DC + 1, :, 1, :], 1.0).then_inc(s_cd, 1)
            v.memset(xnT[DC:DC + 1, 1, :], 1.0).then_inc(s_cd, 1)
            v.memset(vs[:], 0.0).then_inc(s_cd, 1)
            v.memset(wr_sp[:].bitcast(F32), 0.0).then_inc(s_wrs, 1)
            v.memset(thr[:], 0).then_inc(s_cd, 1)
            for k in range(3):
                v.memset(digit[:, k], (k + 1) << (BITS - 2)).then_inc(s_cd, 1)
            dve.wait_ge(s_dw, 16)
            dve.sem_inc(s_mul, FREE)
            dve.sem_inc(s_ye, FREE)

            def conv(b, part):
                for k in [range(1, 2), range(2, 4), range(4, 6), range(6, 7)][part]:
                    for c in range(2):
                        acc, src = cv[0:DC, b.parity, c], xb[:, b.parity, c, k:k + L]
                        if k == 1:
                            dve.wait_ge(s_tap0, b.v * 2 + (c + 1))
                        else:
                            dve.wait_ge(s_conv, b.v * TAP_OPS + (2 * k + c - 3))
                        v.scalar_tensor_tensor(acc, src, dw_sb[:, c, k:k + 1], acc, ALU.mult,
                                               ALU.add).then_inc(s_conv, 1)

            def maxima(b, k):
                dve.wait_ge(s_s, b.v * NG + (k + 1))
                v.tensor_reduce(nmax[:, HG * k:HG * (k + 1)], bank_s[k][:, 0:HG * L].rearrange(
                    "p (h n) -> p h n", h=HG), AX.X, ALU.max, negate=True).then_inc(s_max, 1)

            def inverse(b, k):
                dve.wait_ge(s_exp, b.v * NG + (k + 1))
                if b.after(1):
                    dve.wait_ge(s_norm, b.v * NG + (k + 1 - NG))
                v.reciprocal(rinv[:, HG * k:HG * (k + 1)], rsum[:, HG * k:HG * (k + 1)]).then_inc(s_rinv, 1)

            def keys(b):
                dve.wait_ge(s_kt, b.v + 1)
                if b.after(1):
                    dve.wait_ge(s_s, b.v * NG)
                v.tensor_tensor(kbd[:, 0], kT[:, 0].unsqueeze(1).to_broadcast([DC, 6, L]),
                                headmask[:].unsqueeze(2).to_broadcast([DC, 6, L]), ALU.mult).then_inc(s_kbd, 1)

            def ln1_stats(b):
                dve.wait_ge(s_y, b.v + 1)
                v.bn_stats(st[:, 0], bank_y[:, 0:D]).then_inc(s_ln, 1)
                dve.wait_ge(s_ln, b.v * 7 + 1)
                if b.after(1):
                    dve.wait_ge(s_r1, b.v * 2)
                v.memset(carry[:, 0:1], 0.0)
                v.bn_aggr(mv[:, 0], st[:, 0]).then_inc(s_ln, 1)
                dve.wait_ge(s_ln, b.v * 7 + 2)

            def ln1_apply(b):
                v.scalar_tensor_tensor(tn[:], bank_y[:, 0:D], mv[:, 0, 0:1], g_bc[:], ALU.subtract,
                                       ALU.mult).then_inc(s_ln, 1)
                dve.wait_ge(s_ln, b.v * 7 + 3)
                dve.wait_ge(s_r1, b.v * 2 + 2)
                if b.after(1):
                    dve.wait_ge(s_relu, b.v)
                v.scalar_tensor_tensor(un[:], tn[:], rstd[:, 0], b_bc[:], ALU.mult, ALU.add).then_inc(s_ln, 1)

            def ln2_stats(b):
                dve.wait_ge(s_relu, b.v + 1)
                v.bn_stats(st[:, 1], h1[:]).then_inc(s_ln, 1)
                dve.wait_ge(s_ln, b.v * 7 + 5)
                if b.after(1):
                    dve.wait_ge(s_r2, b.v * 2)
                v.memset(carry[:, 1:2], 0.0)
                v.bn_aggr(mv[:, 1], st[:, 1]).then_inc(s_ln, 1)
                dve.wait_ge(s_ln, b.v * 7 + 6)

            def ln2_apply(b):
                dve.wait_ge(s_r2, b.v * 2 + 2)
                if b.after(1):
                    dve.wait_ge(s_t1, b.v)
                v.tensor_scalar(xn[:], h1[:], mv[:, 1, 0:1], rstd[:, 1], ALU.subtract, ALU.mult).then_inc(s_ln, 1)

            def split_wr():
                dve.wait_ge(s_sw, 48)
                dve.wait_ge(s_wrs, 1)
                v.tensor_copy(wr_sp[:, 0:2, 0:NE], wr_raw[:]).then_inc(s_wrs, 2)
                dve.wait_ge(s_wrs, 3)
                v.tensor_tensor(wr_sp[:, 2:4, 0:NE], wr_raw[:], wr_sp[:, 0:2, 0:NE].bitcast(F32),
                                ALU.subtract).then_inc(s_wrs, 2)

            def lo_rows(b):
                cols = bass.ds(b.v * L, L)
                dve.wait_ge(s_xn2t, b.v + 1)
                v.tensor_tensor(xs[:, LO_A, cols], bank_k[:, 0:L], xs[:, HI_A, cols].bitcast(F32),
                                ALU.subtract).then_inc(s_xlo, 1)
                v.tensor_tensor(xs[DB:128, HI_LO_B, cols], bank_k[DB:128, L:2 * L],
                                xs[DB:128, HI_LO_B, cols].bitcast(F32), ALU.subtract).then_inc(s_xlo, 1)

            def ln3(b):
                row = H[:, bass.ds(b.v, 1)].rearrange("p o d -> p (o d)")
                dve.wait_ge(s_proj, b.v + 1)
                dve.wait_ge(s_h1b, b.v + 1)
                if b.after(1):
                    dve.wait_ge(s_hc, b.v)
                v.tensor_tensor(hrow[:], bank_o[:, 0:D], row, ALU.add).then_inc(s_l3, 1)
                dve.wait_ge(s_l3, b.v * 5 + 1)
                v.bn_stats(st[:, 2], hrow[:]).then_inc(s_l3, 1)
                dve.wait_ge(s_l3, b.v * 5 + 2)
                v.memset(carry[:, 2:3], 0.0)
                v.bn_aggr(mv[:, 2], st[:, 2]).then_inc(s_l3, 1)

            def ln3_apply(b):
                dve.wait_ge(s_l3, b.v * 5 + 3)
                dve.wait_ge(s_r3, b.v * 2 + 2)
                if b.after(1):
                    dve.wait_ge(s_t2, b.v)
                for cols, src in ((slice(0, D), slice(0, D)), (slice(D, DW), slice(DA, D))):
                    v.tensor_scalar(xn2s[:, cols], hrow[:, src], mv[:, 2, 0:1], rstd[:, 2], ALU.subtract,
                                    ALU.mult).then_inc(s_l3, 1)

            def taps(x, parts):
                if x.inside():
                    for part in parts:
                        conv(x, part)

            def step(i):
                a, n, x, m = i, i + 2, i + 4, i + -1
                if i.reg is None and i.const == -2:
                    dve.wait_ge(s_cst, 1)
                    dve.wait_ge(s_bc, 16 * 3)
                    split_wr()
                if a.inside():
                    maxima(a, 0)
                taps(x, [0])
                if a.inside():
                    maxima(a, 1)
                taps(x, [1])
                if (i + -2).inside():
                    lo_rows(i + -2)
                if a.inside():
                    maxima(a, 2)
                    inverse(a, 0)
                    maxima(a, 3)
                    inverse(a, 1)
                if n.inside():
                    ln1_stats(n)
                if a.inside():
                    inverse(a, 2)
                if (i + 1).inside():
                    keys(i + 1)
                if n.inside():
                    ln1_apply(n)
                if a.inside():
                    inverse(a, 3)
                if m.inside():
                    ln3(m)
                if n.inside():
                    ln2_stats(n)
                taps(x, [2])
                if m.inside():
                    ln3_apply(m)
                taps(x, [3])
                if n.inside():
                    ln2_apply(n)

            steps(dve, step)

            chain = [0]

            def link(ins, k=1):
                chain[0] += 1
                ins.then_inc(s_rt, 1)
                dve.wait_ge(s_rt, chain[0])

            def wide(ap):
                return ap.unsqueeze(2).to_broadcast([128, NB, NE])

            def softmax():
                dve.wait_ge(s_lgt, 1)
                lg = turn[0][:, 0:NB * NE].rearrange("p (t e) -> p t e", e=NE)
                link(v.tensor_reduce(RS[0][:], lg, AX.X, ALU.max))
                link(v.tensor_tensor(RT[1][:], lg, wide(RS[0][:]), ALU.subtract))
                dve.wait_ge(s_rex, 1)
                link(v.tensor_reduce(RS[1][:], RT[1][:], AX.X, ALU.add))
                link(v.reciprocal(RS[2][:], RS[1][:]))
                link(v.tensor_tensor(RT[0][:], RT[1][:], wide(RS[2][:]), ALU.mult))

            def best(j):
                link(v.tensor_reduce(RS[j][:], RT[0][:], AX.X, ALU.max))
                link(v.tensor_tensor(RT[1][:], RT[0][:], wide(RS[j][:]), ALU.is_equal))
                link(v.tensor_tensor(RT[1][:], RT[1][:], edesc[:], ALU.mult))
                link(v.tensor_reduce(RS[2][:], RT[1][:], AX.X, ALU.max))
                link(v.tensor_tensor(oh[:, j], edesc[:], wide(RS[2][:]), ALU.is_equal))

            def first_choice():
                best(0)
                link(v.scalar_tensor_tensor(RT[0][:].rearrange("p t e -> p (t e)"),
                                            oh[:, 0].rearrange("p t e -> p (t e)"), -2.0,
                                            RT[0][:].rearrange("p t e -> p (t e)"), ALU.mult, ALU.add))
            def second_choice():
                best(1)
                link(v.tensor_tensor(RS[2][:], RS[0][:], RS[1][:], ALU.add))
                link(v.tensor_scalar(RS[2][:], RS[2][:], 1e-9, None, ALU.max))
                link(v.reciprocal(RS[3][:], RS[2][:]))
                for j in range(2):
                    link(v.tensor_tensor(wgt[:, j], RS[j][:], RS[3][:], ALU.mult))
                    link(v.tensor_tensor(RT[1 + j][:], oh[:, j], wide(wgt[:, j]), ALU.mult))
                link(v.tensor_tensor(RT[3][:], oh[:, 0], oh[:, 1], ALU.add))
                link(v.tensor_tensor(RT[1][:], RT[1][:], RT[2][:], ALU.add))
                link(v.scalar_tensor_tensor(score[:].rearrange("p t e -> p (t e)"),
                                            RT[3][:].rearrange("p t e -> p (t e)"), 1.0,
                                            RT[1][:].rearrange("p t e -> p (t e)"), ALU.subtract, ALU.add))
                v.tensor_copy(xn2[:, :, DW:DW + NE], RT[1][:]).then_inc(s_wt, 1)

            def over(ap):
                return ap.unsqueeze(1).to_broadcast([128, NB, NE])

            def search_count():
                k = len(searched)
                searched.append(k)
                w = 6 * k
                v.tensor_tensor(cand[:], thr[:].unsqueeze(1).to_broadcast([128, 3, NE]), digit[:],
                                ALU.bitwise_or).then_inc(s_thr, 1)
                dve.wait_ge(s_thr, w + 1)
                v.tensor_tensor(above[:], score[:].unsqueeze(1).to_broadcast([128, 3, NB, NE]),
                                cand[:].bitcast(F32).unsqueeze(2).to_broadcast([128, 3, NB, NE]),
                                ALU.is_ge).then_inc(s_thr, 1)
                v.tensor_scalar(digit[:], digit[:], 2, None, ALU.logical_shift_right).then_inc(s_thr, 1)
                dve.wait_ge(s_thr, w + 3)
                v.tensor_reduce(cnt[:], above[:].rearrange("p k t e -> p k e t"), AX.X, ALU.add).then_inc(s_cnt, 1)

            def search_take():
                k = len(searched) - 1
                w = 6 * k
                dve.wait_ge(s_tot, k + 1)
                v.tensor_scalar(reach[:], tot[:], float(CAP), None, ALU.is_ge).then_inc(s_thr, 1)
                dve.wait_ge(s_thr, w + 4)
                with nc.allow_low_precision("counts up to three"):
                    v.tensor_reduce(two[:], reach[:].rearrange("p k e -> p e k"), AX.X, ALU.add).then_inc(s_thr, 1)
                dve.wait_ge(s_thr, w + 5)
                v.scalar_tensor_tensor(thr[:], two[:], BITS - 2 - 2 * k, thr[:], ALU.logical_shift_left,
                                       ALU.bitwise_or).then_inc(s_thr, 1)
                dve.wait_ge(s_thr, w + 6)

            searched = []

            def gated(u, par, c, c0, n, hi=True, lo=False):
                dve.wait_ge(s_silu, u + 1)
                dve.wait_ge(s_lo, u + 1)
                v.tensor_tensor(gf[:, par, 0:n], sg[:, par, 0:n], up_b[par][:, 0:n], ALU.mult).then_inc(s_mul, 1)
                if hi:
                    dve.wait_ge(s_mul, u + (FREE + 1))
                    v.tensor_copy(G[:, 0, c, c0:c0 + n], gf[:, par, 0:n]).then_inc(s_hi, 1)
                if lo:
                    dve.wait_ge(s_hi, u + 1)
                    dve.wait_ge(s_lo, u + FREE)
                    v.tensor_tensor(G[:, 1, c, c0:c0 + n], gf[:, par, 0:n], G[:, 0, c, c0:c0 + n].bitcast(F32),
                                    ALU.subtract).then_inc(s_lo, 1)

            def add_shared(d, par, tile):
                dve.wait_ge(s_d, d + 1)
                row = H[:, tile]
                v.tensor_tensor(row, down[par][:, 0:D], row, ALU.add).then_inc(s_sh, 1)
                dve.wait_ge(s_sh, d + 1)
                v.tensor_tensor(row, down[par][:, D:2 * D], row, ALU.add).then_inc(s_ye, 1)

            def masks():
                t = thr[:].bitcast(F32)
                link(v.tensor_tensor(RT[3][:], score[:], over(t), ALU.is_gt))
                link(v.tensor_reduce(cnt[:, 0], RT[3][:].rearrange("p t e -> p e t"), AX.X, ALU.add))
                v.sem_inc(s_cnt, 1)
                v.tensor_tensor(RT[4][:], score[:], over(t), ALU.is_equal).then_inc(s_pre, 1)

            def ranks(n, mask, res):
                dve.wait_ge(s_lgt, 2 + n)
                by_e = "p t e -> p e t"
                all_p = turn[1][:, 128:128 + NB * NE].rearrange("p (t e) -> p e t", e=NE)
                tr = RT[6][:].rearrange("p t e -> p (t e)").rearrange("p (e t) -> p e t", e=NE)
                flat = "p e t -> p (e t)"
                link(v.tensor_copy(tr, all_p))
                sc = RT[7][:].rearrange("p t e -> p (t e)")
                link(v.tensor_tensor_scan(sc, segm[:].rearrange(flat), tr.rearrange(flat), 0.0, ALU.mult, ALU.add))
                link(v.tensor_tensor(sc, sc, tr.rearrange(flat), ALU.subtract))
                link(v.tensor_tensor(res, turn[1][:, 0:NB * NE].rearrange("p (t e) -> p t e", e=NE),
                                     sc.rearrange("p (e t) -> p t e", e=NE), ALU.add))

            def keep():
                ranks(0, RT[4], RT[1][:])
                dve.wait_ge(s_tot, BITS // 2 + 1)
                link(v.tensor_tensor(RT[1][:], RT[1][:], over(tot[:, 0]), ALU.add))
                link(v.tensor_scalar(RT[1][:], RT[1][:], float(CAP), None, ALU.is_lt))
                link(v.tensor_tensor(RT[1][:], RT[1][:], RT[4][:], ALU.mult))
                link(v.tensor_tensor(RT[5][:], RT[1][:], RT[3][:], ALU.add))
                v.sem_inc(s_pre, 2)

            def slots():
                ranks(1, RT[5], RT[1][:])
                link(v.tensor_tensor(RT[1][:], RT[1][:], ebase[:], ALU.add))

            def place(j):
                link(v.tensor_tensor(RT[2][:], oh[:, j], RT[1][:], ALU.mult))
                link(v.tensor_reduce(RS[0][:], RT[2][:], AX.X, ALU.add))
                link(v.tensor_tensor(RT[2][:], oh[:, j], RT[5][:], ALU.mult))
                link(v.tensor_reduce(RS[1][:], RT[2][:], AX.X, ALU.add))
                link(v.tensor_tensor(RS[0][:], RS[0][:], dump[:, j], ALU.subtract))
                link(v.tensor_tensor(RS[0][:], RS[0][:], RS[1][:], ALU.mult))
                link(v.tensor_tensor(dst_i[:, j], RS[0][:], dump[:, j], ALU.add))
                v.sem_inc(s_ix, 1)

            def slot_info(e):
                p = e.parity
                dve.wait_ge(s_xg[p], e.pair * 16 + 16)
                dve.wait_ge(s_add[p], e.pair * ADDED + 16)
                v.tensor_copy(wslot[:, p], xg[:, p, :, bass.ds(e.v + DW, 1)].rearrange(
                    "p t o -> p (t o)")).then_inc(s_info, 1)
                v.tensor_scalar(unused[:], xg[:, p, :, RW - 1], 0.0, None, ALU.is_equal).then_inc(s_info, 1)
                dve.wait_ge(s_info, e.v * 3 + 2)
                v.tensor_tensor(unused[:], unused[:], spare[:, p], ALU.mult).then_inc(s_unused, 1)
                dve.wait_ge(s_unused, e.v + 1)
                v.tensor_tensor(row_i[:, p], unused[:], xg[:, p, :, RW - 1], ALU.add).then_inc(s_info, 1)

            def turned(e, t):
                p, cols = e.parity, slice(t * 128, (t + 1) * 128)
                bank = turn[(e.const * CT + t) % 2]
                dve.wait_ge(s_xt, e.v * CT + (t + 1))
                v.tensor_copy(xgs[:, p, HI_A:HI_LO_B + 1, cols],
                              bank[:, 0:256].rearrange("p (c n) -> p c n", c=2)).then_inc(s_xhi, 1)
                dve.wait_ge(s_xhi, e.v * CT + (t + 1))
                v.tensor_tensor(xgs[:, p, LO_A, cols], bank[:, 0:128], xgs[:, p, HI_A, cols].bitcast(F32), ALU.subtract)
                v.tensor_tensor(xgs[DB:128, p, HI_LO_B, cols], bank[DB:128, 128:256],
                                xgs[DB:128, p, HI_LO_B, cols].bitcast(F32), ALU.subtract).then_inc(s_xte, 1)

            softmax()
            first_choice()
            for grp in range(SH):
                helped = grp < HELP
                for c in range(IC):
                    search = search_at(grp, chunk=c)
                    if search:
                        search_count()
                    gated(grp * IC + c, c % 2, c, 0, GN, hi=not helped, lo=not helped)
                    if search:
                        search_take()
                    if grp == 0 and c == 0:
                        second_choice()
                for t in range(-1, GT):
                    if t >= 0:
                        add_shared(grp * GT + t, t % 2, grp * GT + t)
                    if search_at(grp, tile=t):
                        search_count()
                        search_take()
                    if grp == SH - 1 and t >= 0:
                        for n in TURN_AT[t]:
                            turned(Tile(0), n)
                    if grp == PLACE:
                        if t == -1:
                            masks()
                            keep()
                        elif t == 0:
                            slots()
                            place(0)
                        elif t == 2:
                            place(1)

            def expert(e, more):
                for hf in range(2):
                    for c in range(IC):
                        gated(e.v * (2 * IC) + (U_E0 + hf * IC + c), c % 2, c, hf * HALF, HALF, lo=hf == 0)
                for t in range(CT):
                    row = ys[:, e.parity, t, :]
                    dve.wait_ge(s_y1, e.v * CT + (t + 1))
                    v.scalar_tensor_tensor(row, down[(e.const * CT + t) % 2][:, D:2 * D],
                                           wslot[:, e.parity, t:t + 1], row, ALU.mult, ALU.add).then_inc(s_ye, 1)
                    if more:
                        for n in TURN_AT[t]:
                            turned(e + 1, n)
                        if t == CT - 2:
                            slot_info(e + 1)

            slot_info(Tile(0))
            with dve.Fori(0, NE // 2 - 1) as r:
                expert(Tile(0, r), True)
                expert(Tile(1, r), True)
            expert(Tile(NE - 2), True)
            expert(Tile(NE - 1), False)


_OUT = (NB, L, D)


def kernel(x, L0_tok_dw_w, L0_tok_pw_w, L0_tok_pw_b, L0_tok_ln_g, L0_tok_ln_b, L0_attn_W_attn,
           L0_attn_b_attn, L0_attn_W_proj, L0_attn_b_proj, L0_ffn_Wr, L0_ffn_w1, L0_ffn_w3, L0_ffn_w2,
           L0_ffn_s1, L0_ffn_s3, L0_ffn_s2):
    import numpy as np
    import concourse.bacc as bacc
    from concourse.bass_utils import run_bass_kernel_spmd

    def chunks(w):
        w = np.asarray(w)
        return np.ascontiguousarray(np.moveaxis(w.reshape(w.shape[:-2] + (2, DC, w.shape[-1])), -3, -2))

    def inner(w):
        w = np.asarray(w)
        return np.ascontiguousarray(np.moveaxis(w.reshape(w.shape[:-2] + (IC, 128, w.shape[-1])), -3, -2))

    x = np.asarray(x)[..., 0]
    pad = (TAPS - 1) // 2
    xp = np.zeros((NB, L + 2 * pad, D), x.dtype)
    xp[:, pad:pad + L] = x
    wp = np.zeros((4, HG, 32, D), x.dtype)
    wp[:, :, 0:HS] = np.asarray(L0_attn_W_proj).reshape(HG, 4, HS, D).transpose(1, 0, 2, 3)
    arrays = {
        "xT": np.ascontiguousarray(xp.transpose(2, 0, 1).reshape(2, DC, NB, L + 2 * pad).transpose(1, 0, 2, 3)),
        "dw": chunks(np.asarray(L0_tok_dw_w).reshape(D, TAPS)),
        "pwT": chunks(np.asarray(L0_tok_pw_w).T),
        "pw_b": np.asarray(L0_tok_pw_b).reshape(1, D),
        "ln_g": np.asarray(L0_tok_ln_g),
        "ln_b": np.asarray(L0_tok_ln_b),
        "wqkv": chunks(L0_attn_W_attn),
        "b_attn": np.asarray(L0_attn_b_attn).reshape(1, 3 * D),
        "wproj": np.ascontiguousarray(wp.transpose(0, 2, 1, 3).reshape(128, HG, D)),
        "b_proj": np.asarray(L0_attn_b_proj),
        "wr": np.asarray(L0_ffn_Wr),
        "w13": np.stack([np.asarray(L0_ffn_w1), np.asarray(L0_ffn_w3)], -2), "w2": inner(L0_ffn_w2),
        "s13": np.stack([np.asarray(L0_ffn_s1), np.asarray(L0_ffn_s3)], -2), "s2": inner(L0_ffn_s2),
    }
    nc = bacc.Bacc("TRN2", target_bir_lowering=False, num_devices=1)
    ins = [nc.dram_tensor(n, a.shape, mybir.dt.from_np(a.dtype), kind="ExternalInput").ap() for n, a in arrays.items()]
    out = nc.dram_tensor("out", _OUT, F32, kind="ExternalOutput").ap()
    vit_tower(nc, *ins, out)
    r = run_bass_kernel_spmd(nc, [arrays], core_ids=[0])
    return r.results[0]["out"]
```
